# Optimizing a Trainium2 kernel written in Bass

```python
import numpy as np
import jax
import jax.numpy as jnp

def _softmax(x, axis=-1):
    return jax.nn.softmax(x, axis=axis)

def _gelu(x):
    return jax.nn.gelu(x, approximate=True)

def _silu(x):
    return jax.nn.silu(x)

def _sigmoid(x):
    return jax.nn.sigmoid(x)

def _layernorm(x, axis=-1, eps=1e-05):
    m = jnp.mean(x, axis=axis, keepdims=True)
    v = jnp.var(x, axis=axis, keepdims=True)
    return (x - m) / jnp.sqrt(v + eps)

def _scatter_add(tgt, idx, src, axis=0):
    return tgt.at[idx].add(src)

def _segment_sum(src, seg, n):
    return jax.ops.segment_sum(src, seg, n)
kernel_name = 'mk_adaln_d1_jaxref_r8_b6ec93'

def setup_inputs(seed: int=0):
    np.random.seed(seed)
    _w = jnp.asarray

    def _L0_attn_setup():
        import jax, jax.numpy as jnp
        import numpy as np
        EMB = 128
        NQ = 16
        NKV = 4
        D = 64
        B, S = (1, 256)
        ROPE_BASE = 10000.0

        def _rotary(t):
            d = t.shape[-1]
            inv_freq = 1.0 / ROPE_BASE ** (jnp.arange(0, d, 2, dtype=jnp.float32) / d)
            pos = jnp.arange(t.shape[1], dtype=jnp.float32)
            ang = pos[:, None] * inv_freq[None, :]
            cos = jnp.concatenate([jnp.cos(ang), jnp.cos(ang)], axis=-1)[None, :, None, :]
            sin = jnp.concatenate([jnp.sin(ang), jnp.sin(ang)], axis=-1)[None, :, None, :]
            x1, x2 = (t[..., :d // 2], t[..., d // 2:])
            t_rot = jnp.concatenate([-x2, x1], axis=-1)
            return t * cos + t_rot * sin
        key = jax.random.key(seed)
        ks = jax.random.split(key, 5)
        std = 0.02
        return {'x': jax.random.normal(ks[0], (B, S, EMB), jnp.float32), 'Wq': jax.random.normal(ks[1], (EMB, NQ * D), jnp.float32) * std, 'bq': jnp.zeros((NQ * D,), jnp.float32), 'Wk': jax.random.normal(ks[2], (EMB, NKV * D), jnp.float32) * std, 'bk': jnp.zeros((NKV * D,), jnp.float32), 'Wv': jax.random.normal(ks[3], (EMB, NKV * D), jnp.float32) * std, 'bv': jnp.zeros((NKV * D,), jnp.float32), 'Wo': jax.random.normal(ks[4], (NQ * D, EMB), jnp.float32) * std, 'bo': jnp.zeros((EMB,), jnp.float32)}
    _L0_attn_in = _L0_attn_setup()

    def _L0_ffn_setup():
        import jax, jax.numpy as jnp
        import numpy as np
        W_SCALE = 0.02
        TOP_K = 2
        key = jax.random.key(seed)
        ks = jax.random.split(key, 5)
        B, S, H, I, E = (2, 128, 128, 512, 8)
        return {'x': jax.random.normal(ks[0], (B, S, H), dtype=jnp.float32), 'gate': jax.random.normal(ks[1], (H, E), dtype=jnp.float32) * W_SCALE, 'experts_w1': jax.random.normal(ks[2], (E, H, I), dtype=jnp.float32) * W_SCALE, 'experts_w2': jax.random.normal(ks[3], (E, I, H), dtype=jnp.float32) * W_SCALE, 'experts_w3': jax.random.normal(ks[4], (E, H, I), dtype=jnp.float32) * W_SCALE}
    _L0_ffn_in = _L0_ffn_setup()
    _L0_c = _w((lambda *s: np.random.randn(*s).astype(np.float32) * 0.05)(1, 128))
    _L0_wmod = _w((lambda *s: np.random.randn(*s).astype(np.float32) * 0.05)(128, 6 * 128) * 128 ** (-0.5))
    _d = {'L0_attn_x': _L0_attn_in['x'], 'L0_attn_Wq': _L0_attn_in['Wq'], 'L0_attn_bq': _L0_attn_in['bq'], 'L0_attn_Wk': _L0_attn_in['Wk'], 'L0_attn_bk': _L0_attn_in['bk'], 'L0_attn_Wv': _L0_attn_in['Wv'], 'L0_attn_bv': _L0_attn_in['bv'], 'L0_attn_Wo': _L0_attn_in['Wo'], 'L0_attn_bo': _L0_attn_in['bo'], 'L0_ffn_gate': _L0_ffn_in['gate'], 'L0_ffn_experts_w1': _L0_ffn_in['experts_w1'], 'L0_ffn_experts_w2': _L0_ffn_in['experts_w2'], 'L0_ffn_experts_w3': _L0_ffn_in['experts_w3'], 'L0_c': _L0_c, 'L0_wmod': _L0_wmod}
    _x0 = _d['L0_attn_x']
    _d['L0_attn_x'] = jax.random.normal(jax.random.fold_in(jax.random.key(seed), 1), (1, 2048, 128), dtype=_x0.dtype)
    del _x0
    return _d

def reference(L0_attn_x, L0_attn_Wq, L0_attn_bq, L0_attn_Wk, L0_attn_bk, L0_attn_Wv, L0_attn_bv, L0_attn_Wo, L0_attn_bo, L0_ffn_gate, L0_ffn_experts_w1, L0_ffn_experts_w2, L0_ffn_experts_w3, L0_c, L0_wmod):

    def _L0_attn_ref(x, Wq, bq, Wk, bk, Wv, bv, Wo, bo):
        import jax, jax.numpy as jnp
        import numpy as np
        EMB = 128
        NQ = 16
        NKV = 4
        D = 64
        B, S = (1, 256)
        ROPE_BASE = 10000.0

        def _rotary(t):
            d = t.shape[-1]
            inv_freq = 1.0 / ROPE_BASE ** (jnp.arange(0, d, 2, dtype=jnp.float32) / d)
            pos = jnp.arange(t.shape[1], dtype=jnp.float32)
            ang = pos[:, None] * inv_freq[None, :]
            cos = jnp.concatenate([jnp.cos(ang), jnp.cos(ang)], axis=-1)[None, :, None, :]
            sin = jnp.concatenate([jnp.sin(ang), jnp.sin(ang)], axis=-1)[None, :, None, :]
            x1, x2 = (t[..., :d // 2], t[..., d // 2:])
            t_rot = jnp.concatenate([-x2, x1], axis=-1)
            return t * cos + t_rot * sin
        b, s, _ = x.shape
        g = NQ // NKV
        q = (x @ Wq + bq).reshape(b, s, NQ, D)
        k = (x @ Wk + bk).reshape(b, s, NKV, D)
        v = (x @ Wv + bv).reshape(b, s, NKV, D)
        q = _rotary(q)
        k = _rotary(k)
        qg = q.reshape(b, s, NKV, g, D)
        scale = 1.0 / jnp.sqrt(jnp.float32(D))
        logits = jnp.einsum('bqhgd,bkhd->bhgqk', qg, k) * scale
        causal = jnp.tril(jnp.ones((s, s), bool))
        logits = jnp.where(causal, logits, jnp.float32(-1e+30))
        w = jax.nn.softmax(logits, axis=-1)
        out = jnp.einsum('bhgqk,bkhd->bqhgd', w, v).reshape(b, s, NQ * D)
        return out @ Wo + bo

    def _L0_ffn_ref(x, gate, experts_w1, experts_w2, experts_w3):
        import jax, jax.numpy as jnp
        import numpy as np
        W_SCALE = 0.02
        TOP_K = 2
        E = experts_w1.shape[0]
        router_logits = jnp.einsum('bsh,he->bse', x, gate)
        routing_weights, selected = jax.lax.top_k(router_logits, TOP_K)
        routing_weights = jax.nn.softmax(routing_weights, axis=-1)
        onehot = jax.nn.one_hot(selected, E, dtype=x.dtype)
        tok_w = jnp.einsum('bsk,bske->bse', routing_weights, onehot)
        g = jnp.einsum('bsh,ehi->ebsi', x, experts_w1)
        u = jnp.einsum('bsh,ehi->ebsi', x, experts_w3)
        hid = jax.nn.silu(g) * u
        eo = jnp.einsum('ebsi,eih->ebsh', hid, experts_w2)
        out = jnp.einsum('ebsh,bse->bsh', eo, tok_w)
        return out
    x = L0_attn_x
    mod = (_silu(L0_c) @ L0_wmod).reshape(L0_c.shape[0], 6, 1, -1)
    sa, ca, ga, sb, cb, gb = (mod[:, 0], mod[:, 1], mod[:, 2], mod[:, 3], mod[:, 4], mod[:, 5])
    ga = (2 * (ga >= 0) - 1) * jnp.maximum(jnp.abs(ga), 0.25)
    gb = (2 * (gb >= 0) - 1) * jnp.maximum(jnp.abs(gb), 0.25)
    h = _layernorm(x, axis=-1) * (1 + ca) + sa
    x = x + ga * _L0_attn_ref(h, L0_attn_Wq, L0_attn_bq, L0_attn_Wk, L0_attn_bk, L0_attn_Wv, L0_attn_bv, L0_attn_Wo, L0_attn_bo)
    h = _layernorm(x, axis=-1) * (1 + cb) + sb
    x = x + gb * _L0_ffn_ref(h, L0_ffn_gate, L0_ffn_experts_w1, L0_ffn_experts_w2, L0_ffn_experts_w3)
    return x

_drawn_inputs = setup_inputs


def setup_inputs(seed=0):
    import zlib

    import numpy as np

    out = dict(_drawn_inputs(seed))
    spreads = {'L0_attn_bq': (0.0, 0.8),
     'L0_attn_bk': (0.0, 0.8),
     'L0_attn_bv': (0.0, 0.536),
     'L0_attn_bo': (0.0, 0.323)}
    factors = {'L0_attn_Wq': 8.0,
     'L0_attn_Wk': 8.0,
     'L0_attn_Wv': 8.0,
     'L0_attn_Wo': 3.813,
     'L0_ffn_gate': 8.0,
     'L0_ffn_experts_w1': 8.0,
     'L0_ffn_experts_w2': 8.0,
     'L0_ffn_experts_w3': 8.0}
    for name, (base, spread) in spreads.items():
        noise = np.random.default_rng([zlib.crc32(name.encode()), seed]).standard_normal(out[name].shape)
        drawn = base * np.exp(spread * noise) if base else spread * noise
        out[name] = jnp.asarray(drawn.astype(out[name].dtype))
    for name, factor in factors.items():
        out[name] = (out[name] * factor).astype(out[name].dtype)
    return out
```

```python
from contextlib import ExitStack

import numpy as np

import concourse.bass as bass
from concourse import mybir

ALU = mybir.AluOpType
ACT = mybir.ActivationFunctionType
AX = mybir.AxisListType
F32 = mybir.dt.float32
F32R = mybir.dt.float32r
BF16 = mybir.dt.bfloat16

P = 128
BANK = 512
HEAD = 64
HALF = HEAD // 2
LN_EPS = 1e-5
GATE_FLOOR = 0.25
MASKED = -1e30
ROPE_BASE = 10000.0


def rotary_tables(tokens):
    inv_freq = (1.0 / np.float32(ROPE_BASE) ** (np.arange(0, HEAD, 2, dtype=np.float32) / np.float32(HEAD)))
    angle = np.arange(tokens, dtype=np.float32)[:, None] * inv_freq.astype(np.float32)[None, :]
    cos, sin = np.cos(angle).astype(np.float32), np.sin(angle).astype(np.float32)
    return np.concatenate([cos, cos], 1), np.concatenate([-sin, sin], 1)


def constants(tokens, experts):
    cos, sin = rotary_tables(tokens)
    row, col = np.arange(P)[:, None], np.arange(P)[None, :]
    earlier = np.arange(experts)[None, :] < np.arange(experts)[:, None]
    return {
        "k_cos": cos,
        "k_sin": sin,
        "k_ident": np.eye(P, dtype=np.float32),
        "k_causal": np.where(col <= row, 0.0, MASKED).astype(np.float32),
        "k_earlier": np.broadcast_to(earlier.astype(np.float32).reshape(1, -1), (P, experts * experts)).copy(),
    }


def block_kernel(nc, x, Wq, bq, Wk, bk, Wv, bv, Wo, bo, gate, w1, w2, w3, c, wmod,
                 cos, sin, ident_in, causal_in, earlier_in, out):
    T, E = x.shape[1], x.shape[2]
    GROUPS = Wk.shape[1] // HEAD
    QH = Wq.shape[1] // HEAD // GROUPS
    PAIRS = QH // 2
    TILES = T // P
    QK = (QH + 1) * HEAD
    QKV = QK + HEAD
    NX, INNER = w1.shape[0], w1.shape[2]
    IT = INNER // P
    TB = BANK // P
    CHUNKS = TILES // TB
    SCALE = float(HEAD) ** -0.5
    assert E == P and SCALE == 0.125

    STEPS = TILES * QH

    def banks(s):
        return s // QH // TB + 1

    def cols(s):
        return (s // QH + 1) * P

    def base(s):
        return 0 if banks(s) > 2 else 2 * (s % 2)

    slots, slot_at, engine_of = [], {}, []

    def add_slot(key, engine):
        slot_at[key] = len(slots)
        slots.append(key)
        engine_of.append(engine)

    def transpose_engine(s, g):
        if banks(s) == 1:
            return "act" if s % 2 else "dve"
        return "act" if g == 0 else "dve"

    add_slot(("proj", 0), "dve")
    add_slot(("tq", 0), "act")
    add_slot(("tk", 0), "dve")
    for s in range(STEPS):
        i, h = divmod(s, QH)
        if h == 0 and i + 1 < TILES:
            add_slot(("proj", i + 1), "dve")
        for g in range(banks(s)):
            add_slot(("p", s, g), transpose_engine(s, g))
        if h == 2 and i + 1 < TILES:
            add_slot(("tq", i + 1), "act")
            add_slot(("tk", i + 1), "dve")
        if h == 3 and i > 0:
            add_slot(("wo", i - 1), "dve")
    add_slot(("wo", TILES - 1), "dve")

    def emptied_by(n):
        return engine_of[n], sum(1 for m in range(n + 1) if engine_of[m] == engine_of[n])

    with ExitStack() as ctx:
        def sb(name, shape, dt=F32):
            return ctx.enter_context(nc.sbuf_tensor(name, shape, dt))

        def sem(name):
            return ctx.enter_context(nc.semaphore(name))

        PS = ctx.enter_context(nc.psum_tensor("PS", [P, 8, BANK], F32))
        RING, AV = 4, 6

        ident = sb("ident", [P, P])
        ident16 = sb("ident16", [P, P], BF16)
        causal = sb("causal", [P, P])
        causal16 = sb("causal16", [P, P], BF16)
        earlier = sb("earlier", [P, NX, NX])
        cos_sb = sb("cos_sb", [P, TILES, HEAD])
        sin_sb = sb("sin_sb", [P, TILES, HEAD])
        wqkv = sb("wqkv", [P, GROUPS, QKV])
        bqkv = sb("bqkv", [P, GROUPS, QKV])
        wo_sb = sb("wo_sb", [P, GROUPS, PAIRS, E])
        bo_sb = sb("bo_sb", [P, E])
        wmod_sb = sb("wmod_sb", [P, 6 * E])
        c_sb = sb("c_sb", [P, 1])
        silu_c = sb("silu_c", [P, P])
        gate_sb = sb("gate_sb", [P, NX])
        modcol = sb("modcol", [P, 4])
        gates = sb("gates", [P, 2, E])
        gate_abs = sb("gate_abs", [P, 2, E])
        gate_sign = sb("gate_sign", [P, 2, E])
        gate_bo = sb("gate_bo", [P, E])
        X = sb("X", [P, TILES, E])
        XA = sb("XA", [P, TILES, E])
        hT = sb("hT", [P, TILES, P])
        stats = sb("stats", [P, TILES, 6])
        moments = sb("moments", [P, TILES, 2])
        rstd = sb("rstd", [P, TILES])
        qkv_sb = sb("qkv_sb", [P, 2, QK])
        rot_cos = sb("rot_cos", [P, QK])
        rot_sin = sb("rot_sin", [P, QK])
        rotated = sb("rotated", [P, QK])
        q_split = sb("q_split", [P, 2, QH, 2, HEAD], F32R)
        k_split = sb("k_split", [P, 2, 2, 2, HEAD], F32R)
        QT = sb("QT", [P, 2, QH, P], F32R)
        KT = sb("KT", [P, 2, T], F32R)
        V = sb("V", [P, TILES, HEAD])
        probs = sb("probs", [P, 2, T])
        PT = sb("PT", [P, 4, TILES, P])
        top = sb("top", [P, 4, 2])
        neg_max = sb("neg_max", [P, 4])
        row_sum = sb("row_sum", [P, 4])
        inv_sum = sb("inv_sum", [P, 2, 2, HEAD])
        inv_sumT = sb("inv_sumT", [P, 2, P])
        attnT = sb("attnT", [P, 2, PAIRS, P])
        w1_sb = sb("w1_sb", [P, 2, INNER])
        w3_sb = sb("w3_sb", [P, 2, INNER])
        w2_sb = sb("w2_sb", [P, 2, IT, E])
        w2_gated = sb("w2_gated", [P, 2, IT, E])
        silu_g = sb("silu_g", [P, 2, BANK])
        hidden = PT[:, 0:2, :, :].rearrange("p b (i t) k -> p b i (t k)", t=TB)
        logits = sb("logits", [P, TILES, NX])
        rank_gt = sb("rank_gt", [P, TILES, NX, NX])
        rank_eq = sb("rank_eq", [P, TILES, NX, NX])
        rank = sb("rank", [P, TILES, NX])
        best = sb("best", [P, TILES])
        tok_w = sb("tok_w", [P, TILES, NX])
        tok_sum = sb("tok_sum", [P, TILES])
        tok_wT = sb("tok_wT", [P, NX, TILES])

        ld_x, ld_mod, ld_const, ld_attn = sem("ld_x"), sem("ld_mod"), sem("ld_const"), sem("ld_attn")
        dve_chain, silu_c_ready, mod_filled, mod_ready = (
            sem("dve_chain"), sem("silu_c_ready"), sem("mod_filled"), sem("mod_ready"))
        var_ready, std_ready, norm_ready = sem("var_ready"), sem("std_ready"), sem("norm_ready")
        norm_transposed, hT_ready = sem("norm_transposed"), sem("hT_ready")
        setup_done = sem("setup_done")
        proj_added, pool_chain, rotated_ready = sem("proj_added"), sem("pool_chain"), sem("rotated_ready")
        scores_head, scores_ready, max_chain, max_ready = (
            sem("scores_head"), sem("scores_ready"), sem("max_chain"), sem("max_ready"))
        probs_ready, ring_filled, ring_act, ring_dve = (
            sem("probs_ready"), sem("ring_filled"), sem("ring_act"), sem("ring_dve"))
        inv_ready, pv_ready, invT_ready, attn_ready = (
            sem("inv_ready"), sem("pv_ready"), sem("invT_ready"), sem("attn_ready"))
        engine_through, group_go = sem("engine_through"), sem("group_go")
        router_filled, logits_ready, exp_logits, tok_w_ready = (
            sem("router_filled"), sem("logits_ready"), sem("exp_logits"), sem("tok_w_ready"))
        ld_w = [sem("ld_w0"), sem("ld_w1")]
        w2_ready = sem("w2_ready")
        gu_filled, silu_ready, hidden_ready = sem("gu_filled"), sem("silu_ready"), sem("hidden_ready")
        y_filled, y_added = sem("y_filled"), sem("y_added")
        stored = sem("stored")

        block = ctx.enter_context(nc.Block())

        n_act = sum(1 for e in engine_of if e == "act")
        n_dve = len(slots) - n_act
        POOL_OPS = 7
        n_max_chain = sum(1 for s in range(STEPS) if banks(s) > 1)
        LOOP_SEMS = [
            (proj_added, TILES), (pool_chain, POOL_OPS * TILES), (rotated_ready, TILES),
            (scores_head, n_max_chain), (scores_ready, STEPS), (max_chain, 2 * n_max_chain),
            (max_ready, STEPS), (probs_ready, STEPS), (ring_filled, len(slots)), (ring_act, n_act),
            (ring_dve, n_dve), (inv_ready, STEPS // 2), (pv_ready, STEPS // 2),
            (invT_ready, STEPS // 2), (attn_ready, STEPS // 2),
        ]
        ring_sem = {"act": ring_act, "dve": ring_dve}

        def ring_bank(n, width):
            return PS[:, RING + n % 2, 0:width]

        UNITS = CHUNKS * IT

        @block.sync
        def _(sp):
            sp.dma_start(X[:], x[0].rearrange("(i p) e -> p i e", p=P)).then_inc(ld_x, 16)
            sp.dma_start(wmod_sb[:], wmod).then_inc(ld_mod, 16)
            sp.dma_start(c_sb[:], c.rearrange("a e -> e a")).then_inc(ld_mod, 16)
            sp.dma_start(ident[:], ident_in).then_inc(ld_const, 16)
            sp.dma_start(causal[:], causal_in).then_inc(ld_const, 16)
            sp.dma_start(bo_sb[:], bo.partition_broadcast(P)).then_inc(ld_const, 16)
            sp.dma_start(wo_sb[:], Wo.rearrange("(g j p) e -> p g j e", p=P, j=PAIRS)).then_inc(ld_const, 16)
            q_cols, k_cols = slice(0, QH * HEAD), slice(QH * HEAD, QK)
            for m, (w, b, at) in enumerate(((Wq, bq, q_cols), (Wk, bk, k_cols), (Wv, bv, slice(QK, QKV)))):
                sp.dma_start(wqkv[:, :, at], w.rearrange("e (g n) -> e g n", g=GROUPS)).then_inc(ld_attn, 16)
                sp.dma_start(bqkv[:, :, at], b.rearrange("(g n) -> g n", g=GROUPS).partition_broadcast(P))\
                  .then_inc(ld_attn, 16)
            sp.dma_start(cos_sb[:], cos.rearrange("(i p) d -> p i d", p=P)).then_inc(ld_attn, 16)
            sp.dma_start(sin_sb[:], sin.rearrange("(i p) d -> p i d", p=P)).then_inc(ld_attn, 16)
            sp.dma_start(gate_sb[:], gate).then_inc(ld_attn, 16)
            sp.dma_start(earlier[:].rearrange("p a b -> p (a b)"), earlier_in).then_inc(ld_attn, 16)

            def load_expert(e, b):
                sp.dma_start(w1_sb[:, b, :], w1[bass.ds(e, 1)].rearrange("o h i -> h (o i)")).then_inc(ld_w[b], 16)
                sp.dma_start(w3_sb[:, b, :], w3[bass.ds(e, 1)].rearrange("o h i -> h (o i)")).then_inc(ld_w[b], 16)
                sp.dma_start(w2_sb[:, b, :, :], w2[bass.ds(e, 1)].rearrange("o (t p) h -> p (o t) h", p=P))\
                  .then_inc(ld_w[b], 16)

            for b in range(2):
                load_expert(b, b)

            with sp.Fori(0, GROUPS) as g:
                for s, count in LOOP_SEMS:
                    sp.wait_ge(s, count)
                sp.wait_ge(engine_through, 4)
                for s, _ in LOOP_SEMS:
                    sp.sem_clear(s)
                sp.sem_clear(engine_through)
                sp.sem_inc(group_go, 1)

            with sp.Fori(0, NX // 2 - 1) as turn:
                e0 = turn * 2
                for b in range(2):
                    sp.wait_ge(y_filled, (e0 + b + 1) * CHUNKS)
                    load_expert(e0 + 2 + b, b)
            sp.wait_ge(y_added, NX * TILES)
            sp.dma_start(out[0].rearrange("(i p) e -> p i e", p=P), XA[:]).then_inc(stored, 16)
            sp.wait_ge(stored, 16)

        @block.gpsimd
        def _(pool):
            chain = [0]

            def link(ins):
                chain[0] += 1
                ins.then_inc(pool_chain, 1)
                return chain[0]

            def gate_w2(b):
                nc.gpsimd.tensor_tensor(w2_gated[:, b], w2_sb[:, b],
                                        gates[:, 1:2, :].broadcast_to([P, IT, E]), ALU.mult).then_inc(w2_ready, 1)

            pool.wait_ge(mod_ready, 1)
            for b in range(2):
                pool.wait_ge(ld_w[b], 48)
                gate_w2(b)
            pool.wait_ge(ld_attn, 160)
            with pool.Fori(0, GROUPS) as g:
                chain[0] = 0
                for i in range(TILES):
                    b = i % 2
                    pool.wait_ge(proj_added, i + 1)
                    qk = qkv_sb[:, b, :].rearrange("p (h n) -> p h n", n=HEAD)
                    cs = cos_sb[:, i:i + 1, :].broadcast_to([P, QH + 1, HEAD])
                    rc = rot_cos[:].rearrange("p (h n) -> p h n", n=HEAD)
                    rs = rot_sin[:].rearrange("p (h n) -> p h n", n=HEAD)
                    ro = rotated[:].rearrange("p (h n) -> p h n", n=HEAD)
                    link(nc.gpsimd.tensor_tensor(rc, qk, cs, ALU.mult))
                    for lo, hi in ((0, HALF), (HALF, HEAD)):
                        sn = sin_sb[:, i:i + 1, lo:hi].broadcast_to([P, QH + 1, HALF])
                        done = link(nc.gpsimd.tensor_tensor(
                            rs[:, :, lo:hi], qk[:, :, HALF - lo:HEAD - lo], sn, ALU.mult))
                    pool.wait_ge(pool_chain, done)
                    nc.gpsimd.tensor_tensor(ro, rc, rs, ALU.add)
                    nc.gpsimd.tensor_tensor(q_split[:, b, :, 0, :], rc[:, 0:QH], rs[:, 0:QH], ALU.add)
                    for m in range(2):
                        last = nc.gpsimd.tensor_tensor(k_split[:, b, 0, m, :], rc[:, QH], rs[:, QH], ALU.add)
                    done = link(last)
                    pool.wait_ge(pool_chain, done)
                    link(nc.gpsimd.tensor_tensor(q_split[:, b, :, 1, :], ro[:, 0:QH],
                                                 q_split[:, b, :, 0, :].bitcast(F32), ALU.subtract))
                    for m in range(2):
                        last = nc.gpsimd.tensor_tensor(k_split[:, b, 1, m, :], ro[:, QH],
                                                       k_split[:, b, 0, m, :].bitcast(F32), ALU.subtract)
                        done = link(last)
                    assert chain[0] == POOL_OPS * (i + 1)
                    pool.wait_ge(pool_chain, done)
                    pool.sem_inc(rotated_ready, 1)
                pool.sem_inc(engine_through, 1)
                pool.wait_ge(group_go, g + 1)

            with pool.Fori(0, NX // 2 - 1) as turn:
                e0 = turn * 2
                for b in range(2):
                    pool.wait_ge(ld_w[b], e0 * 24 + 96)
                    pool.wait_ge(y_filled, (e0 + b + 1) * CHUNKS)
                    gate_w2(b)

        @block.scalar
        def _(act):
            act.wait_ge(ld_mod, 32)
            nc.scalar.activation(silu_c[:], c_sb[:, 0:1].broadcast_to([P, P]), ACT.Silu).then_inc(silu_c_ready, 1)

            def norm(k):
                act.wait_ge(var_ready, k + 1)
                nc.scalar.activation(rstd[:], moments[:, :, 1], ACT.Sqrt).then_inc(std_ready, 1)
                if k == 0:
                    act.wait_ge(mod_ready, 1)
                for r in range(CHUNKS):
                    act.wait_ge(norm_transposed, k * CHUNKS + r + 1)
                    nc.scalar.activation(hT[:, r * TB:(r + 1) * TB, :].rearrange("p a b -> p (a b)"), PS[:, r, :],
                                         ACT.Identity, bias=modcol[:, 2 * k:2 * k + 1],
                                         scale=modcol[:, 2 * k + 1:2 * k + 2]).then_inc(hT_ready, 1)

            norm(0)

            def ring_to(dst, n, width, scale=1.0):
                act.wait_ge(ring_filled, n + 1)
                nc.scalar.activation(dst, ring_bank(n, width), ACT.Copy, scale=scale).then_inc(ring_act, 1)

            def softmax(s):
                act.wait_ge(max_ready, s + 1)
                if s >= 4:
                    act.wait_ge(inv_ready, s // 2 - 1)
                nc.scalar.activation(probs[:, s % 2, 0:cols(s)],
                                     PS[:, base(s):base(s) + banks(s), :].rearrange("p b n -> p (b n)")[:, 0:cols(s)],
                                     ACT.Exp, bias=neg_max[:, s % 4:s % 4 + 1],
                                     accum_out=row_sum[:, s % 4:s % 4 + 1]).then_inc(probs_ready, 1)

            def queries(i):
                n = slot_at[("tq", i)]
                ring_to(QT[:, i % 2].rearrange("p h n -> p (h n)"), n, QH * P, scale=SCALE)

            def inverse_sums(pr):
                act.wait_ge(pv_ready, pr + 1)
                if pr >= 2:
                    act.wait_ge(attn_ready, pr - 1)
                nc.scalar.copy(inv_sumT[:, pr % 2, :], PS[:, AV + pr % 2, P:2 * P]).then_inc(invT_ready, 1)

            with act.Fori(0, GROUPS) as g:
                queries(0)
                softmax(0)
                for s in range(STEPS):
                    i, h = divmod(s, QH)
                    mine = [gr for gr in range(banks(s)) if transpose_engine(s, gr) == "act"]
                    for gr in mine:
                        if s >= 4:
                            act.wait_ge(pv_ready, s // 2 - 1)
                        width = min(TB, i + 1 - gr * TB) * P
                        ring_to(PT[:, s % 4, gr * TB:gr * TB + width // P, :].rearrange("p a b -> p (a b)"),
                                slot_at[("p", s, gr)], width)
                    if s + 1 < STEPS:
                        softmax(s + 1)
                    if s % 2 == 0 and s >= 4:
                        inverse_sums(s // 2 - 2)
                    if h == 2 and i + 1 < TILES:
                        queries(i + 1)
                inverse_sums(STEPS // 2 - 2)
                inverse_sums(STEPS // 2 - 1)
                act.sem_inc(engine_through, 1)
                act.wait_ge(group_go, g + 1)

            norm(1)
            act.wait_ge(logits_ready, 1)
            nc.scalar.activation(tok_w[:], logits[:], ACT.Exp).then_inc(exp_logits, 1)

            with act.Fori(0, NX // 2) as turn:
                e0 = turn * 2
                for u in range(2 * UNITS):
                    act.wait_ge(gu_filled, e0 * UNITS + u + 1)
                    nc.scalar.activation(silu_g[:, u % 2, :], PS[:, 2 * (u % 2), :], ACT.Silu).then_inc(silu_ready, 1)

        @block.vector
        def _(dve):
            chain = [0]

            def link(ins):
                chain[0] += 1
                ins.then_inc(dve_chain, 1)
                dve.wait_ge(dve_chain, chain[0])

            def norm(k, source):
                for i in range(TILES):
                    last = nc.vector.bn_stats(stats[:, i, :], source[:, i, :])
                link(last)
                for i in range(TILES):
                    last = nc.vector.bn_aggr(moments[:, i, :], stats[:, i, :])
                link(last)
                nc.vector.tensor_scalar(moments[:, :, 1], moments[:, :, 1], LN_EPS, None, ALU.add)\
                  .then_inc(var_ready, 1)
                dve.wait_ge(std_ready, k + 1)
                link(nc.vector.reciprocal(rstd[:], rstd[:]))
                for i in range(TILES):
                    last = nc.vector.tensor_scalar(X[:, i, :], source[:, i, :], moments[:, i, 0:1], rstd[:, i:i + 1],
                                                   ALU.subtract, ALU.mult)
                    if i % TB == TB - 1:
                        last.then_inc(norm_ready, 1)

            dve.wait_ge(mod_filled, 1)
            ga_gb = PS[:, 4:6, 2 * E:3 * E]
            link(nc.vector.tensor_copy(gates[:], ga_gb))
            link(nc.vector.scalar_tensor_tensor(out=gate_abs[:], in0=gates[:], scalar=-1.0, in1=gates[:],
                                                op0=ALU.mult, op1=ALU.max))
            nc.vector.tensor_scalar(gate_abs[:], gate_abs[:], GATE_FLOOR, None, ALU.max)
            nc.vector.tensor_scalar(gate_sign[:], ga_gb, 0.0, 2.0, ALU.is_ge, ALU.mult)
            nc.vector.tensor_copy(modcol[:, 0:4:2], PS[:, 6, 0:4:2])
            link(nc.vector.tensor_scalar(modcol[:, 1:4:2], PS[:, 6, 1:4:2], 1.0, None, ALU.add))
            link(nc.vector.scalar_tensor_tensor(out=gates[:], in0=gate_sign[:], scalar=-1.0, in1=gate_abs[:],
                                                op0=ALU.add, op1=ALU.mult))
            dve.wait_ge(ld_const, 64)
            nc.vector.tensor_copy(ident16[:], ident[:])
            nc.vector.tensor_copy(causal16[:], causal[:])
            link(nc.vector.tensor_tensor(gate_bo[:], gates[:, 0, :], bo_sb[:], ALU.mult)) 
            dve.wait_ge(ld_x, 16)
            nc.vector.tensor_tensor(XA[:], X[:], gate_bo[:].unsqueeze(1).broadcast_to([P, TILES, E]), ALU.add)
            for g in range(GROUPS):
                last = nc.vector.tensor_tensor(wo_sb[:, g], wo_sb[:, g],
                                               gates[:, 0:1, :].broadcast_to([P, PAIRS, E]), ALU.mult)
            link(last)
            dve.sem_inc(mod_ready, 1)
            norm(0, X)
            dve.wait_ge(ld_attn, 160)

            def maximum(s):
                if banks(s) > 1:
                    nb = banks(s)
                    dve.wait_ge(scores_head, n_head(s))
                    nc.vector.reduce_max(top[:, s % 4, 0:1],
                                         PS[:, base(s):base(s) + nb - 1, :].rearrange("p b n -> p (b n)"), AX.X)\
                      .then_inc(max_chain, 1)
                    dve.wait_ge(scores_ready, s + 1)
                    nc.vector.reduce_max(top[:, s % 4, 1:2],
                                         PS[:, base(s) + nb - 1, 0:cols(s) - BANK * (nb - 1)], AX.X)\
                      .then_inc(max_chain, 1)
                    dve.wait_ge(max_chain, 2 * n_head(s))
                    nc.vector.tensor_scalar(neg_max[:, s % 4:s % 4 + 1], top[:, s % 4, 0:1], top[:, s % 4, 1:2], -1.0,
                                            ALU.max, ALU.mult).then_inc(max_ready, 1)
                else:
                    dve.wait_ge(scores_ready, s + 1)
                    nc.vector.reduce_max(neg_max[:, s % 4:s % 4 + 1], PS[:, base(s), 0:cols(s)], AX.X, negate=True)\
                      .then_inc(max_ready, 1)

            def n_head(s):
                return sum(1 for t in range(s + 1) if banks(t) > 1)

            def ring_wait(key):
                dve.wait_ge(ring_filled, slot_at[key] + 1)
                return slot_at[key]

            def project(i, g):
                n = ring_wait(("proj", i))
                if i >= 2:
                    dve.wait_ge(rotated_ready, i - 1)
                nc.vector.tensor_tensor(qkv_sb[:, i % 2, :], ring_bank(n, QK),
                                        bqkv[:, bass.ds(g, 1), 0:QK].rearrange("p o n -> p (o n)"), ALU.add)\
                  .then_inc(proj_added, 1)
                nc.vector.tensor_tensor(V[:, i, :], PS[:, RING + n % 2, QK:QKV],
                                        bqkv[:, bass.ds(g, 1), QK:QKV].rearrange("p o n -> p (o n)"), ALU.add)\
                  .then_inc(ring_dve, 1)

            def keys(i):
                n = ring_wait(("tk", i))
                nc.vector.tensor_copy(KT[:, :, i * P:(i + 1) * P], ring_bank(n, 2 * P).rearrange("p (a b) -> p a b", a=2))\
                  .then_inc(ring_dve, 1)

            def residual(i):
                n = ring_wait(("wo", i))
                nc.vector.tensor_tensor(XA[:, i, :], XA[:, i, :], ring_bank(n, E), ALU.add).then_inc(ring_dve, 1)

            def normalise(pr):
                dve.wait_ge(invT_ready, pr + 1)
                i, j = divmod(pr, PAIRS)
                nc.vector.tensor_tensor(attnT[:, i % 2, j, :], PS[:, AV + pr % 2, 0:P], inv_sumT[:, pr % 2, :],
                                        ALU.mult).then_inc(attn_ready, 1)

            with dve.Fori(0, GROUPS) as g:
                project(0, g)
                keys(0)
                maximum(0)
                for s in range(STEPS):
                    i, h = divmod(s, QH)
                    if h == 0 and i + 1 < TILES:
                        project(i + 1, g)
                    if s + 1 < STEPS:
                        maximum(s + 1)
                    mine = [gr for gr in range(banks(s)) if transpose_engine(s, gr) == "dve"]
                    if mine and s >= 4:
                        dve.wait_ge(pv_ready, s // 2 - 1)
                    for gr in mine:
                        width = min(TB, i + 1 - gr * TB) * P
                        n = ring_wait(("p", s, gr))
                        nc.vector.tensor_copy(PT[:, s % 4, gr * TB:gr * TB + width // P, :].rearrange("p a b -> p (a b)"),
                                              ring_bank(n, width)).then_inc(ring_dve, 1)
                    if s % 2:
                        k = 2 * (s // 2 % 2)
                        dve.wait_ge(probs_ready, s + 1)
                        nc.vector.reciprocal(inv_sum[:, s // 2 % 2], row_sum[:, k:k + 2].unsqueeze(2).broadcast_to([P, 2, HEAD]))\
                            .then_inc(inv_ready, 1)
                    elif s >= 4:
                        normalise(s // 2 - 2)
                    if h == 2 and i + 1 < TILES:
                        keys(i + 1)
                    if h == 3 and i > 0:
                        residual(i - 1)
                normalise(STEPS // 2 - 2)
                normalise(STEPS // 2 - 1)
                residual(TILES - 1)
                dve.sem_inc(engine_through, 1)
                dve.wait_ge(group_go, g + 1)

            norm(1, XA)
            dve.wait_ge(router_filled, 1)
            link(nc.vector.tensor_copy(logits[:], PS[:, 4, 0:TILES * NX].rearrange("p (t x) -> p t x", x=NX)))
            mine_x = logits[:].unsqueeze(3).broadcast_to([P, TILES, NX, NX])
            other = logits[:].unsqueeze(2).broadcast_to([P, TILES, NX, NX])
            nc.vector.reduce_max(best[:], logits[:], AX.X)
            for t in range(TILES):
                nc.vector.tensor_tensor(rank_gt[:, t], other[:, t], mine_x[:, t], ALU.is_gt)
                last = nc.vector.tensor_tensor(rank_eq[:, t], other[:, t], mine_x[:, t], ALU.is_equal)
            link(last)
            for t in range(TILES):
                last = nc.vector.tensor_tensor(rank_eq[:, t], rank_eq[:, t], earlier[:], ALU.mult)
            nc.vector.tensor_tensor(logits[:], logits[:], best[:].unsqueeze(2).broadcast_to([P, TILES, NX]),
                                    ALU.subtract).then_inc(logits_ready, 1)
            link(last)
            link(nc.vector.tensor_tensor(rank_gt[:].rearrange("p t a b -> p (t a b)"),
                                         rank_gt[:].rearrange("p t a b -> p (t a b)"),
                                         rank_eq[:].rearrange("p t a b -> p (t a b)"), ALU.add))
            link(nc.vector.tensor_reduce(rank[:].rearrange("p t x -> p (t x)"),
                                         rank_gt[:].rearrange("p t a b -> p (t a) b"), AX.X, ALU.add))
            dve.wait_ge(exp_logits, 1)
            link(nc.vector.scalar_tensor_tensor(out=tok_w[:], in0=rank[:], scalar=1.5, in1=tok_w[:],
                                                op0=ALU.is_lt, op1=ALU.mult))
            link(nc.vector.reduce_sum(tok_sum[:], tok_w[:], AX.X))
            link(nc.vector.reciprocal(tok_sum[:], tok_sum[:]))
            link(nc.vector.tensor_tensor(tok_wT[:].rearrange("p x t -> p t x"), tok_w[:],
                                         tok_sum[:].unsqueeze(2).broadcast_to([P, TILES, NX]), ALU.mult))

            def gate_up(e0, u):
                dve.wait_ge(silu_ready, e0 * UNITS + u + 1)
                ch, it = divmod(u, IT)
                nc.vector.tensor_tensor(hidden[:, ch % 2, it, :], silu_g[:, u % 2, :], PS[:, 2 * (u % 2) + 1, :],
                                        ALU.mult).then_inc(hidden_ready, 1)

            def add_expert(e0, ch):
                dve.wait_ge(y_filled, e0 * CHUNKS + ch + 1)
                e = e0 + ch // CHUNKS
                for t in range(TB):
                    i = ch % CHUNKS * TB + t
                    nc.vector.scalar_tensor_tensor(
                        out=XA[:, i, :], in0=PS[:, 4 + ch % 2, t * P:(t + 1) * P],
                        scalar=tok_wT[:, bass.ds(e, 1), i:i + 1].rearrange("p o t -> p (o t)"), in1=XA[:, i, :],
                        op0=ALU.mult, op1=ALU.add).then_inc(y_added, 1)

            with dve.Fori(0, NX // 2) as turn:
                e0 = turn * 2
                for ch in range(2 * CHUNKS):
                    for it in range(IT):
                        gate_up(e0, ch * IT + it)
                        if it == 1 and ch >= 1:
                            add_expert(e0, ch - 1)
                add_expert(e0, 2 * CHUNKS - 1)

        @block.tensor
        def _(pe):
            pe.wait_ge(ld_mod, 32)
            pe.wait_ge(silu_c_ready, 1)
            for m in range(2):
                nc.tensor.matmul(PS[:, 4 + m, 0:3 * E], silu_c[:], wmod_sb[:, 3 * m * E:3 * (m + 1) * E],
                                 start=True, stop=True)
            for n, m in enumerate((0, 1, 3, 4)):
                last = nc.tensor.matmul(PS[:, 6, n:n + 1], wmod_sb[:, m * E:(m + 1) * E], silu_c[:, 0:1],
                                        start=True, stop=True)
            last.then_inc(mod_filled, 1)

            def norm(k):
                if k == 0:
                    pe.wait_ge(ld_const, 64)
                for r in range(CHUNKS):
                    pe.wait_ge(norm_ready, k * CHUNKS + r + 1)
                    for t in range(TB):
                        last = nc.tensor.transpose(PS[:, r, t * P:(t + 1) * P], X[:, r * TB + t, :], ident[:])
                    last.then_inc(norm_transposed, 1)

            norm(0)
            pe.wait_ge(ld_attn, 160)
            pe.wait_ge(hT_ready, CHUNKS)

            def ring_free(n):
                if n >= 2:
                    engine, count = emptied_by(n - 2)
                    pe.wait_ge(ring_sem[engine], count)

            def project(i, g):
                n = slot_at[("proj", i)]
                ring_free(n)
                nc.tensor.matmul(ring_bank(n, QKV), hT[:, i, :], wqkv[:, bass.ds(g, 1), :].rearrange("p o n -> p (o n)"),
                                 start=True, stop=True).then_inc(ring_filled, 1)

            def split_transposes(i):
                pe.wait_ge(rotated_ready, i + 1)
                n = slot_at[("tq", i)]
                ring_free(n)
                for h in range(QH):
                    last = nc.tensor.transpose(PS[:, RING + n % 2, h * P:(h + 1) * P],
                                               q_split[:, i % 2, h].rearrange("p a b -> p (a b)").bitcast(F32), ident[:])
                last.then_inc(ring_filled, 1)
                n = slot_at[("tk", i)]
                ring_free(n)
                for m in range(2):
                    last = nc.tensor.transpose(PS[:, RING + n % 2, m * P:(m + 1) * P],
                                               k_split[:, i % 2, m].rearrange("p a b -> p (a b)").bitcast(F32), ident[:])
                last.then_inc(ring_filled, 1)

            def scores(s):
                i, h = divmod(s, QH)
                if h == 0:
                    for key in (("tq", i), ("tk", i)):
                        engine, count = emptied_by(slot_at[key])
                        pe.wait_ge(ring_sem[engine], count)
                users = [t for t in range(max(0, s - 2), s)
                         if base(t) < base(s) + banks(s) and base(s) < base(t) + banks(t)]
                if users:
                    pe.wait_ge(probs_ready, users[-1] + 1)
                for b in range(banks(s)):
                    w = min(BANK, cols(s) - b * BANK)
                    last_bank = b == banks(s) - 1
                    o = PS[:, base(s) + b, 0:w]
                    nc.tensor.matmul(o, QT[:, i % 2, h, :], KT[:, 0, b * BANK:b * BANK + w], start=True, stop=False)
                    last = nc.tensor.matmul(o, QT[:, i % 2, h, :], KT[:, 1, b * BANK:b * BANK + w],
                                            start=False, stop=not last_bank)
                    if last_bank:
                        last = nc.tensor.matmul(PS[:, base(s) + b, w - P:w], ident16[:], causal16[:],
                                                start=False, stop=True)
                    if b == banks(s) - 2:
                        last.then_inc(scores_head, 1)
                last.then_inc(scores_ready, 1)

            def pv(pr, lo, hi, n):
                if lo == 0 and pr >= 2:
                    pe.wait_ge(attn_ready, pr - 1)
                for kt in range(lo, hi):
                    for m in range(2):
                        nc.tensor.matmul(PS[HEAD * m:HEAD * (m + 1), AV + pr % 2, 0:P], V[:, kt, :],
                                         PT[:, (2 * pr + m) % 4, kt, :], start=(kt == 0), stop=(kt == n - 1))

            def pv_finish(pr):
                pe.wait_ge(inv_ready, pr + 1)
                nc.tensor.transpose(PS[:, AV + pr % 2, P:2 * P],
                                    inv_sum[:, pr % 2].rearrange("p a b -> p (a b)"), ident[:])\
                  .then_inc(pv_ready, 1)

            def out_product(i):
                n = slot_at[("wo", i)]
                ring_free(n)
                pe.wait_ge(attn_ready, PAIRS * (i + 1))
                for j in range(PAIRS):
                    last = nc.tensor.matmul(ring_bank(n, E), attnT[:, i % 2, j, :],
                                            wo_sb[:, bass.ds(g_now[0], 1), j, :].rearrange("p o n -> p (o n)"),
                                            start=(j == 0), stop=(j == PAIRS - 1))
                last.then_inc(ring_filled, 1)

            def pt_ready(s):
                per = {}
                for gr in range(banks(s)):
                    engine, count = emptied_by(slot_at[("p", s, gr)])
                    per[engine] = count
                for engine, count in per.items():
                    pe.wait_ge(ring_sem[engine], count)

            g_now = [None]
            with pe.Fori(0, GROUPS) as g:
                g_now[0] = g
                project(0, g)
                split_transposes(0)
                scores(0)
                for s in range(STEPS):
                    i, h = divmod(s, QH)
                    if h == 0 and i + 1 < TILES:
                        project(i + 1, g)
                    if s + 1 < STEPS:
                        scores(s + 1)
                    pr = s // 2 - 1
                    lo = hi = n = 0
                    if pr >= 0:
                        n = pr // PAIRS + 1
                        lo, hi = (0, (n + 1) // 2) if s % 2 == 0 else ((n + 1) // 2, n)
                        if s % 2 == 0:
                            pt_ready(2 * pr)
                            pt_ready(2 * pr + 1)
                    pe.wait_ge(probs_ready, s + 1)
                    for gr in range(banks(s)):
                        m = slot_at[("p", s, gr)]
                        ring_free(m)
                        for t in range(min(TB, i + 1 - gr * TB)):
                            last = nc.tensor.transpose(PS[:, RING + m % 2, t * P:(t + 1) * P],
                                                       probs[:, s % 2, (gr * TB + t) * P:(gr * TB + t + 1) * P], ident[:])
                        last.then_inc(ring_filled, 1)
                        if pr >= 0:
                            a = lo + (hi - lo) * gr // banks(s)
                            z = lo + (hi - lo) * (gr + 1) // banks(s)
                            if z > a:
                                pv(pr, a, z, n)
                    if s % 2 and pr >= 0:
                        pv_finish(pr)
                    if h == 2 and i + 1 < TILES:
                        split_transposes(i + 1)
                    if h == 3 and i > 0:
                        out_product(i - 1)
                pr = STEPS // 2 - 1
                pt_ready(2 * pr)
                pt_ready(2 * pr + 1)
                pv(pr, 0, TILES, TILES)
                pv_finish(pr)
                out_product(TILES - 1)
                pe.sem_inc(engine_through, 1)
                pe.wait_ge(group_go, g + 1)

            norm(1)
            pe.wait_ge(hT_ready, 2 * CHUNKS)
            for i in range(TILES):
                last = nc.tensor.matmul(PS[:, 4, i * NX:(i + 1) * NX], hT[:, i, :], gate_sb[:], start=True, stop=True)
            last.then_inc(router_filled, 1)
            pe.wait_ge(logits_ready, 1)

            def gate_up(e0, u):
                b, it, ch = u // UNITS, u % IT, u % UNITS // IT
                if u % UNITS == 0:
                    pe.wait_ge(ld_w[b], e0 * 24 + 48)
                if u >= 2:
                    pe.wait_ge(hidden_ready, e0 * UNITS + u - 1)
                for m, w in enumerate((w1_sb, w3_sb)):
                    last = nc.tensor.matmul(PS[:, 2 * (u % 2) + m, :], w[:, b, it * P:(it + 1) * P],
                                            hT[:, ch * TB:(ch + 1) * TB, :].rearrange("p a b -> p (a b)"),
                                            start=True, stop=True)
                last.then_inc(gu_filled, 1)

            def down(e0, ch):
                b = ch // CHUNKS
                if ch % CHUNKS == 0:
                    pe.wait_ge(w2_ready, e0 + b + 1)
                pe.wait_ge(hidden_ready, e0 * UNITS + (ch + 1) * IT)
                if ch >= 2:
                    pe.wait_ge(y_added, e0 * TILES + (ch - 1) * TB)
                for t in range(TB):
                    for it in range(IT):
                        last = nc.tensor.matmul(PS[:, 4 + ch % 2, t * P:(t + 1) * P],
                                                hidden[:, ch % 2, it, t * P:(t + 1) * P], w2_gated[:, b, it, :],
                                                start=(it == 0), stop=(it == IT - 1))
                last.then_inc(y_filled, 1)

            with pe.Fori(0, NX // 2) as turn:
                e0 = turn * 2
                for ch in range(2 * CHUNKS):
                    for it in range(IT):
                        gate_up(e0, ch * IT + it)
                        if it == 1 and ch >= 1:
                            down(e0, ch - 1)
                down(e0, 2 * CHUNKS - 1)


_INS = ["L0_attn_x", "L0_attn_Wq", "L0_attn_bq", "L0_attn_Wk", "L0_attn_bk", "L0_attn_Wv", "L0_attn_bv",
        "L0_attn_Wo", "L0_attn_bo", "L0_ffn_gate", "L0_ffn_experts_w1", "L0_ffn_experts_w2",
        "L0_ffn_experts_w3", "L0_c", "L0_wmod"]
_OUTS = [((1, 2048, 128), "float32")]


def kernel(**inputs):
    import numpy as _np
    import concourse.bacc as _bacc
    from concourse import mybir as _mybir
    from concourse.bass_utils import run_bass_kernel_spmd as _run

    nc = _bacc.Bacc("TRN2", target_bir_lowering=False, num_devices=1)
    arrays, args = {}, []
    laid = {name: _np.ascontiguousarray(inputs[name]) for name in _INS}
    laid.update(constants(_OUTS[0][0][1], laid["L0_ffn_gate"].shape[1]))
    for name, a in laid.items():
        arrays[f"in_{name}_dram"] = a
        args.append(nc.dram_tensor(f"in_{name}_dram", a.shape, _mybir.dt.from_np(a.dtype), kind="ExternalInput").ap())
    for i, (shape, dtype) in enumerate(_OUTS):
        dt = _mybir.dt.from_np(_np.dtype(dtype))
        args.append(nc.dram_tensor(f"out_{i}_dram", shape, dt, kind="ExternalOutput").ap())
    block_kernel(nc, *args)
    r = _run(nc, [arrays], core_ids=[0])
    return r.results[0]["out_0_dram"]
```

```python
from contextlib import ExitStack

import numpy as np

import concourse.bass as bass
from concourse import mybir

ALU = mybir.AluOpType
ACT = mybir.ActivationFunctionType
AX = mybir.AxisListType
F32 = mybir.dt.float32
F32R = mybir.dt.float32r
BF16 = mybir.dt.bfloat16

P = 128
BANK = 512
HEAD = 64
HALF = HEAD // 2
LN_EPS = 1e-5
GATE_FLOOR = 0.25
MASKED = -1e30
ROPE_BASE = 10000.0


def rotary_tables(tokens):
    inv_freq = (1.0 / np.float32(ROPE_BASE) ** (np.arange(0, HEAD, 2, dtype=np.float32) / np.float32(HEAD)))
    angle = np.arange(tokens, dtype=np.float32)[:, None] * inv_freq.astype(np.float32)[None, :]
    cos, sin = np.cos(angle).astype(np.float32), np.sin(angle).astype(np.float32)
    return cos, np.concatenate([-sin, sin], 1)


def constants(tokens):
    cos, sin = rotary_tables(tokens)
    row, col = np.arange(P)[:, None], np.arange(P)[None, :]
    return {
        "k_cos": cos,
        "k_sin": sin,
        "k_ident": np.eye(P, dtype=np.float32),
        "k_causal": np.stack([np.where(col <= row, 0.0, MASKED), np.where(row <= col, 0.0, MASKED)], 1)
        .astype(np.float32),
    }


def block_kernel(nc, x_in, Wq, bq, Wk, bk, Wv, bv, Wo, bo, gate, w1, w2, w3, c, wmod,
                 cos, sin, ident_in, causal_in, out):
    T, E = x_in.shape[1], x_in.shape[2]
    GROUPS = Wk.shape[1] // HEAD
    QH = Wq.shape[1] // HEAD // GROUPS
    PAIRS = QH // 2
    TILES = T // P
    QK = (QH + 1) * HEAD
    QKV = QK + HEAD
    NX, INNER = w1.shape[0], w1.shape[2]
    IT = INNER // P
    TB = BANK // P
    SCORE_BANKS, RING_BANKS = 3, 3
    CHUNKS = TILES // TB
    SCALE = float(HEAD) ** -0.5
    assert E == P and SCALE == 0.125 and QH == 4

    PAIR_STEPS = range(CHUNKS * PAIRS)
    N_J = CHUNKS * PAIRS

    def weight(x):
        if x[0] in ("s", "max"):
            _, J, m, t, b = x if x[0] == "max" else (x[0], x[1], x[4], x[3], x[2])
            part = 1.0 if b < J % N_J // PAIRS else ((t + 1) if x[0] == "max" else (TB - t)) / TB
            return part * (2.8 if x[0] == "max" else 2.0)
        return {"pv": 2.1, "qmax": 2.0, "proj": 3.0, "low": 3.0, "qk": 3.5, "poolsum": 0.01, "maxed": 0.5, "diagsum": 3.3, "quadsum": 0.01, "sum": 2.8,
                "rowsum": 7.0, "norm": 2.8, "modulation": 0.0, "out": 8.0}[x[0]]

    def maxima(J, m):
        return [("max", J, m, t, b) for t in range(TB) for b in range(J % N_J // PAIRS + 1)] + [("maxed", J, m)]

    def max_steps(J):
        first, second = maxima(J, 0), maxima(J, 1)
        return first + second[:3] + [("qmax", J, 0)] + second[3:]

    def parts(ch):
        i = ch * TB
        return [("proj", i), ("proj", i + 1), ("low", i), ("proj", i + 2), ("low", i + 1), ("proj", i + 3),
                ("low", i + 2), ("low", i + 3)]

    def turned(ch):
        return [("qk", ch * TB + t) for t in range(TB)]

    def tail_steps(J):
        steps = [("sum", J, m, piece) for m in range(2) for piece in range(3)]
        steps += [("rowsum", J), ("norm", J)]
        return steps + ([("out", J // PAIRS)] if J % PAIRS == PAIRS - 1 else [])

    def diag_steps(J):
        if J // PAIRS == CHUNKS - 1:
            return [("diagsum", J, m, part) for m in range(2) for part in range(2)]
        return [("poolsum", J, m, J // PAIRS) for m in range(2)]

    main = []
    starts, pending = [], []
    for J in PAIR_STEPS:
        starts.append(len(main))
        for q in range(J // PAIRS + 1):
            for r in range(TB):
                main += [("s", J, q, r, 0), ("s", J, q, r, 1)] + pending
                if r == 0 and q > 1:
                    if q < CHUNKS - 1:
                        main += [("poolsum", J, m, q - 1) for m in range(2)]
                    else:
                        main += [("quadsum", J, m, part) for m in range(2) for part in range(4)]
                pending = [("pv", J, q, r)]
    starts.append(len(main))
    before = np.cumsum([0.0] + [weight(x) for x in main])
    begin = [float(before[k]) for k in starts]
    begin.append(begin[-1] + 30.0)

    def place(items, lo, hi):
        at = [begin[int(x)] + (x % 1) * (begin[int(x) + 1] - begin[int(x)]) for x in (lo, hi)]
        ends = np.cumsum([weight(x) for x in items])
        return [(at[0] + (at[1] - at[0]) * float(end - weight(x) / 2) / float(ends[-1]), x)
                for x, end in zip(items, ends)]

    def merge(*placed):
        return [x for _, x in sorted((y for items in placed for y in items), key=lambda y: y[0])]

    end = N_J
    side = [
        place(maxima(2, 0), 0.100, 1.000),
        place([("qmax", 2, 0)] + maxima(2, 1), 1.000, 1.900),
        place(parts(2), 0.600, 2.586), place(turned(2), 2.545, 3.048), place(parts(3), 3.000, 4.000), place(turned(3), 4.342, 5.142),
        place(max_steps(3), 2.039, 2.900), place(max_steps(4), 2.943, 3.893), place(max_steps(5), 4.050, 4.900),
        place(max_steps(6), 4.892, 5.742), place(max_steps(7), 6.057, 6.781),
        place(parts(CHUNKS), 6.200, 7.000), place(turned(CHUNKS), 7.300, 7.433), place(max_steps(end), 7.400, 7.700),
        place(parts(CHUNKS + 1), 7.395, 7.950), place(maxima(end + 1, 0) + maxima(end + 1, 1), 7.807, 7.872),
        place([("qmax", end, 1)], 7.798, 7.733),
        place(turned(CHUNKS + 1), 8.000, 8.400), place([("qmax", end + 1, m) for m in range(2)], 8.400, 8.700),
        place(diag_steps(5), 6.000, 6.100), place(tail_steps(5), 6.250, 6.436),
        place(diag_steps(6) + tail_steps(6), 7.000, 7.450),
        place(tail_steps(-1), 0.020, 0.900), place(diag_steps(7), 8.100, 8.400),
    ] + [place([("qmax", J, 1)], J - 0.020, J - 0.010) for J in range(2, N_J)]\
      + [place(diag_steps(J), J + 1.021, J + 1.100) for J in range(5)]\
      + [place(tail_steps(J), J + 1.350, J + 1.838) for J in range(5)]
    closing = tail_steps(-1)
    body = [("values",)] + merge([(float(b), x) for b, x in zip(before, main)], [(begin[end], x) for x in pending],
                                 *side)
    first = parts(CHUNKS)
    lead_in = first[:4] + [("modulation",)] + first[4:] + turned(CHUNKS) + merge(
        place(max_steps(end) + [("qmax", end, 1)] + max_steps(end + 1) + [("qmax", end + 1, 1)], 0.0, 1.0), place(parts(CHUNKS + 1), 0.0, 1.0)) + turned(CHUNKS + 1)

    class Counts:

        def __init__(self, order):
            self.order = order
            self.at = {}
            number = {}
            for x in order:
                self.at[x] = number.setdefault(x[0], 0)
                number[x[0]] += 1
            self.number = number
            self.slot_at, self.engine_of = {}, []
            for x in order:
                for key, engine in {
                    "proj": [(x, "dve")], "qk": [(("q",) + x[1:], "act"), (("k",) + x[1:], "act")],
                    "max": [(x, "dve")], "qmax": [(x, "act")], "rowsum": [(x, "dve")],
                    "out": [(x, "dve")],
                }.get(x[0], []):
                    self.slot_at[key] = len(self.engine_of)
                    self.engine_of.append(engine)
            self.vector_links = sum((x[0] == "maxed" and x[1] % N_J >= PAIRS)
                                    + (x[0] == "sum" and x[1] not in range(PAIRS) and x[3] == 1) + 2 * (x[0] == "rowsum")
                                    for x in order)

        def emptied(self, key):
            n = self.slot_at[key]
            return self.engine_of[n], self.engine_of[:n + 1].count(self.engine_of[n])

    def acc_quad(J, m):
        J = J % N_J
        return quad_of[J, m, max(J // PAIRS - 1, 0)] % QUADS

    QUADS = 7
    quad_of, quad_owner = {}, []
    for x in body:
        if x[0] == "s" and x[3] == 0:
            _, J, q, _, m = x
            if q < J // PAIRS or q == 0:
                quad_of[J, m, q] = len(quad_owner)
                quad_owner.append((J, m, q))

    assert len(quad_owner) % QUADS == 0

    with ExitStack() as ctx:
        def sb(name, shape, dt=F32):
            return ctx.enter_context(nc.sbuf_tensor(name, shape, dt))

        def sem(name):
            return ctx.enter_context(nc.semaphore(name))

        PS = ctx.enter_context(nc.psum_tensor("PS", [P, 8, BANK], F32))
        SCORES, RING, AV = 0, 3, 6

        ident = sb("ident", [P, P])
        ident16 = sb("ident16", [P, P], BF16)
        causal16 = sb("causal16", [P, 2, P], BF16)
        cos_sb = sb("cos_sb", [P, TILES, HALF])
        sin_sb = sb("sin_sb", [P, TILES, HEAD])
        wqkv = sb("wqkv", [P, GROUPS + 1, QKV])
        bqkv = sb("bqkv", [P, GROUPS + 1, QKV])
        wo_sb = sb("wo_sb", [P, 1 + GROUPS, PAIRS, E])
        c_sb = sb("c_sb", [P, 1])
        ones = sb("ones", [P, HEAD])
        gate_sb = sb("gate_sb", [P, NX])
        modcol = sb("modcol", [P, 4])
        gates = sb("gates", [P, 2, E])
        XA = sb("XA", [P, TILES, E])
        hT = sb("hT", [P, TILES, P])
        stats = sb("stats", [P, TILES, 6])
        moments = sb("moments", [P, TILES, 2])
        rstd = sb("rstd", [P, TILES])
        qkv_sb = sb("qkv_sb", [P, 2, QK])
        rot_cos = sb("rot_cos", [P, QK])
        rot_sin = sb("rot_sin", [P, QK])
        rotated = sb("rotated", [P, 2, QK])
        q_split = sb("q_split", [P, TB, QH, 2, HEAD], F32R)
        k_split = sb("k_split", [P, TB, 2, P], F32R)
        q_max = sb("q_max", [P, 2, TB, QH, P], F32R)
        QT = sb("QT", [P, 2, QH, BANK], F32R)
        QMT = sb("QMT", [P, QH, BANK], F32R)
        KT = sb("KT", [P, 2, T], F32R)
        V = sb("V", [P, TILES, HEAD])
        V_next = sb("V_next", [P, 2 * TB, HEAD])
        part_max = sb("part_max", [P, TB, CHUNKS])
        sum_cols = sb("sum_cols", [P, BANK])
        inv_cols = sb("inv_cols", [P, BANK // 32])
        inv_rows = sb("inv_rows", [P, BANK])
        attnT = sb("attnT", [P, PAIRS, BANK])
        full = sb("full", [P, QUADS, TB, BANK])
        diag = sb("diag", [P, 2, TB, BANK])
        X = full[:, 0].rearrange("p a b -> p (a b)").rearrange("p (i e) -> p i e", e=E)
        normed = [full[:, n].rearrange("p a b -> p (a b)").rearrange("p (i e) -> p i e", e=E)
                  for n in (3, 0)]
        wmod_sb = full[:, 1].rearrange("p a b -> p (a b)")[:, 0:6 * E]
        causal = full[:, 2, 0, 0:2 * P].rearrange("p (a b) -> p a b", b=P)
        silu_c, bo_sb, gate_bo = (full[:, 2, 1, n * P:(n + 1) * P] for n in range(3))
        gate_abs, gate_sign = (full[:, 2, 2, n * 2 * E:(n + 1) * 2 * E].rearrange("p (a b) -> p a b", b=E)
                               for n in range(2))
        hidden = full[:, 1:3]
        weights = full[:, 3:5].rearrange("p n a b -> p n (a b)")
        w1_sb, w3_sb = weights[:, :, 0:INNER], weights[:, :, INNER:2 * INNER]
        w2_sb = weights[:, :, 2 * INNER:2 * INNER + IT * E].rearrange("p n (t e) -> p n t e", e=E)
        w2_gated = weights[:, :, 3 * INNER:3 * INNER + IT * E].rearrange("p n (t e) -> p n t e", e=E)
        silu_g = full[:, 5, 0:2, :]
        hT_hi, hT_lo = KT[:, 0, :], KT[:, 1, :]
        w1_parts = QT[:, 0].rearrange("p (n a) b -> p n a b", a=2)
        w3_parts = QMT[:].rearrange("p (n a) b -> p n a b", a=2)
        beats = full[:, 6].rearrange("p a b -> p (a b)")[:, 0:TILES * NX * NX]\
            .rearrange("p (t a b) -> p t a b", a=NX, b=NX)
        logits, rank, tok_w = (full[:, 5, 3, n * TILES * NX:(n + 1) * TILES * NX]
                               .rearrange("p (t x) -> p t x", x=NX) for n in range(3))
        best = sb("best", [P, TILES])
        tok_sum = sb("tok_sum", [P, TILES])
        tok_wT = sb("tok_wT", [P, NX, TILES])

        ld_x, ld_mod, ld_const, ld_attn = (
            sem("ld_x"), sem("ld_mod"), sem("ld_const"), sem("ld_attn"))
        dve_chain, silu_c_ready, mod_filled, mod_ready = (
            sem("dve_chain"), sem("silu_c_ready"), sem("mod_filled"), sem("mod_ready"))
        var_ready, std_ready, norm_ready = sem("var_ready"), sem("std_ready"), sem("norm_ready")
        norm_transposed, hT_ready = sem("norm_transposed"), sem("hT_ready")
        q_scaled, masks_ready, modcol_ready = sem("q_scaled"), sem("masks_ready"), sem("modcol_ready")
        proj_added, pool_chain, rotated_ready, pool_added = (
            sem("proj_added"), sem("pool_chain"), sem("rotated_ready"), sem("pool_added"))
        ring_filled, ring_act, ring_dve, vector_chain = (
            sem("ring_filled"), sem("ring_act"), sem("ring_dve"), sem("vector_chain"))
        max_ready, scores_ready, probs_ready, pv_done = (
            sem("max_ready"), sem("scores_ready"), sem("probs_ready"), sem("pv_done"))
        diag_added, sum_ready, attn_ready = sem("diag_added"), sem("sum_ready"), sem("attn_ready")
        quad_added = sem("quad_added")
        engine_through, group_go, pads_ready, values_ready = (
            sem("engine_through"), sem("group_go"), sem("pads_ready"), sem("values_ready"))
        parts_ready, low_ready, q_max_ready = sem("parts_ready"), sem("low_ready"), sem("q_max_ready")
        router_filled, logits_ready, exp_logits, tok_w_ready = (
            sem("router_filled"), sem("logits_ready"), sem("exp_logits"), sem("tok_w_ready"))
        ld_w = [sem("ld_w0"), sem("ld_w1")]
        w2_ready, w13_ready = sem("w2_ready"), sem("w13_ready")
        hT_rounded, hT_split, w_rounded = sem("hT_rounded"), sem("hT_split"), sem("w_rounded")
        gu_filled, silu_ready, hidden_ready = sem("gu_filled"), sem("silu_ready"), sem("hidden_ready")
        y_filled, y_added = sem("y_filled"), sem("y_added")
        stored = sem("stored")

        block = ctx.enter_context(nc.Block())

        POOL_OPS = 4
        def loop_sems(n):
            k = n.number
            return [
                (proj_added, k.get("proj", 0)), (pool_chain, POOL_OPS * k.get("proj", 0)),
                (rotated_ready, k.get("proj", 0)), (pool_added, k.get("poolsum", 0)),
                (diag_added, k.get("diagsum", 0) // 2),
                (quad_added, k.get("quadsum", 0) // TB),
                (ring_filled, len(n.engine_of)), (ring_act, n.engine_of.count("act")),
                (ring_dve, n.engine_of.count("dve")), (vector_chain, n.vector_links),
                (max_ready, k.get("maxed", 0)), (scores_ready, k.get("s", 0)), (probs_ready, k.get("s", 0)),
                (pv_done, k.get("pv", 0)), (sum_ready, k.get("sum", 0) // 3),
                (attn_ready, k.get("norm", 0)), (values_ready, k.get("values", 0)),
                (parts_ready, k.get("low", 0)), (low_ready, k.get("low", 0)), (q_max_ready, k.get("low", 0)),
            ]

        ring_sem = {"act": ring_act, "dve": ring_dve}

        lead, loop, last_out = Counts(lead_in), Counts(body), Counts(closing)

        UNITS = CHUNKS * IT

        @block.sync
        def _(sp):
            sp.dma_start(X[:], x_in[0].rearrange("(i p) e -> p i e", p=P)).then_inc(ld_x, 16)
            sp.dma_start(wmod_sb[:], wmod).then_inc(ld_mod, 16)
            sp.dma_start(c_sb[:], c.rearrange("a e -> e a")).then_inc(ld_mod, 16)
            sp.dma_start(ident[:], ident_in).then_inc(ld_const, 16)
            sp.dma_start(causal[:], causal_in).then_inc(ld_const, 16)
            sp.dma_start(bo_sb[:], bo.partition_broadcast(P)).then_inc(ld_const, 16)
            wo_g = Wo.rearrange("(g j p) e -> p g j e", p=P, j=PAIRS)
            sp.dma_start(wo_sb[:, 1:1 + GROUPS], wo_g).then_inc(ld_const, 16)
            sp.dma_start(wo_sb[:, 0:1], wo_g[:, 0:1]).then_inc(ld_const, 16)
            q_cols, k_cols = slice(0, QH * HEAD), slice(QH * HEAD, QK)
            for m, (w, b, at) in enumerate(((Wq, bq, q_cols), (Wk, bk, k_cols), (Wv, bv, slice(QK, QKV)))):
                w_g, b_g = w.rearrange("e (g n) -> e g n", g=GROUPS), b.rearrange("(g n) -> g n", g=GROUPS)
                for lo, n in ((0, GROUPS), (GROUPS, 1)):
                    sp.dma_start(wqkv[:, lo:lo + n, at], w_g[:, 0:n]).then_inc(ld_attn, 16)
                    sp.dma_start(bqkv[:, lo:lo + n, at], b_g[0:n].partition_broadcast(P)).then_inc(ld_attn, 16)
            sp.dma_start(cos_sb[:], cos.rearrange("(i p) d -> p i d", p=P)).then_inc(ld_attn, 16)
            sp.dma_start(sin_sb[:], sin.rearrange("(i p) d -> p i d", p=P)).then_inc(ld_attn, 16)
            sp.dma_start(gate_sb[:], gate).then_inc(ld_attn, 16)

            def load_expert(e, b):
                sp.dma_start(w1_sb[:, b, :], w1[bass.ds(e, 1)].rearrange("o h i -> h (o i)")).then_inc(ld_w[b], 16)
                sp.dma_start(w3_sb[:, b, :], w3[bass.ds(e, 1)].rearrange("o h i -> h (o i)")).then_inc(ld_w[b], 16)
                sp.dma_start(w2_sb[:, b, :, :], w2[bass.ds(e, 1)].rearrange("o (t p) h -> p (o t) h", p=P))\
                  .then_inc(ld_w[b], 16)

            def end_walk(n):
                for s, count in loop_sems(n):
                    if count:
                        sp.wait_ge(s, count)
                sp.wait_ge(engine_through, 4)
                for s, count in loop_sems(n):
                    if count:
                        sp.sem_clear(s)
                sp.sem_clear(engine_through)
                sp.sem_inc(group_go, 1)

            end_walk(lead)
            with sp.Fori(0, GROUPS) as g:
                end_walk(loop)

            for b in range(2):
                load_expert(b, b)

            with sp.Fori(0, NX // 2 - 1) as turn:
                e0 = turn * 2
                for b in range(2):
                    sp.wait_ge(y_filled, (e0 + b + 1) * CHUNKS)
                    load_expert(e0 + 2 + b, b)
            sp.wait_ge(y_added, NX * TILES)
            sp.dma_start(out[0].rearrange("(i p) e -> p i e", p=P), XA[:]).then_inc(stored, 16)
            sp.wait_ge(stored, 16)

        @block.gpsimd
        def _(pool):
            chain = [0]

            def link(ins):
                chain[0] += 1
                ins.then_inc(pool_chain, 1)
                return chain[0]

            nc.gpsimd.memset(ones[:], 1.0)
            nc.gpsimd.memset(k_split[:, :, 1, HEAD:HEAD + 1].bitcast(F32), 1.0)
            nc.gpsimd.memset(k_split[:, :, 1, HEAD + 1:P].bitcast(F32), 0.0)
            nc.gpsimd.memset(q_max[:, :, :, :, HEAD + 1:P].bitcast(F32), 0.0)
            for r in range(1, TB):
                last = nc.gpsimd.memset(diag[:, :, r, 0:r * P], 0.0)
            for m in range(2):
                nc.gpsimd.memset(full[:, acc_quad(-1, m)], 1.0)
            last = nc.gpsimd.memset(attnT[:], 0.0)
            last.then_inc(pads_ready, 1)
            pool.wait_ge(ld_attn, 240)
            def walk(n, ends):
                chain[0] = 0
                for x in n.order:
                    if x[0] == "proj":
                        rotary(n, x)
                    elif x[0] == "poolsum":
                        _, J, m, q = x
                        ch = J // PAIRS
                        if q > 1:
                            pool.wait_ge(pool_added, n.at["poolsum", J, m, q - 1] + 1)
                        if q < ch:
                            pool.wait_ge(pv_done, n.at["pv", J, q, TB - 1] + 1)
                            a, b = quad_of[J, m, q] % QUADS, quad_of[J, m, q - 1] % QUADS
                            nc.gpsimd.tensor_tensor(full[:, a], full[:, a], full[:, b], ALU.add)\
                              .then_inc(pool_added, 1)
                            continue
                        pool.wait_ge(probs_ready, n.at["s", J, ch, TB - 1, m] + 1)
                        acc = full[:, acc_quad(J, m)]
                        if ch:
                            pool.wait_ge(pv_done, n.at["pv", J, ch - 1, TB - 1] + 1)
                            for r in range(TB):
                                last = nc.gpsimd.tensor_tensor(acc[:, r, r * P:BANK], acc[:, r, r * P:BANK],
                                                               diag[:, m, r, r * P:BANK], ALU.add)
                        else:
                            for r in range(0, TB, 2):
                                last = nc.gpsimd.tensor_tensor(acc[:, r // 2, r * P:BANK], diag[:, m, r, r * P:BANK],
                                                               diag[:, m, r + 1, r * P:BANK], ALU.add)
                        last.then_inc(pool_added, 1)
                pool.sem_inc(engine_through, 1)
                pool.wait_ge(group_go, ends)

            def rotary(n, x):
                i = x[1] % TILES
                pool.wait_ge(proj_added, n.at[x] + 1)
                if n.at[x] >= 2:
                    pool.wait_ge(low_ready, n.at[x] - 1)
                    pool.wait_ge(q_max_ready, n.at[x] - 1)
                qk = qkv_sb[:, i % 2, :].rearrange("p (h n) -> p h n", n=HEAD)
                rc = rot_cos[:].rearrange("p (h n) -> p h n", n=HEAD)
                rs = rot_sin[:].rearrange("p (h n) -> p h n", n=HEAD)
                ro = rotated[:, i % 2].rearrange("p (h n) -> p h n", n=HEAD)
                halves = 2 * (QH + 1)
                link(nc.gpsimd.tensor_tensor(rot_cos[:].rearrange("p (h n) -> p h n", n=HALF),
                                             qkv_sb[:, i % 2, :].rearrange("p (h n) -> p h n", n=HALF),
                                             cos_sb[:, i:i + 1, :].broadcast_to([P, halves, HALF]), ALU.mult))
                for lo, hi in ((0, HALF), (HALF, HEAD)):
                    sn = sin_sb[:, i:i + 1, lo:hi].broadcast_to([P, QH + 1, HALF])
                    done = link(nc.gpsimd.tensor_tensor(rs[:, :, lo:hi], qk[:, :, HALF - lo:HEAD - lo], sn, ALU.mult))
                pool.wait_ge(pool_chain, done)
                done = link(nc.gpsimd.tensor_tensor(ro, rc, rs, ALU.add))
                assert chain[0] == POOL_OPS * (n.at[x] + 1)
                pool.wait_ge(pool_chain, done)
                pool.sem_inc(rotated_ready, 1)

            walk(lead, 1)
            with pool.Fori(0, GROUPS) as g:
                walk(loop, g + 2)

            def gate_w2(b):
                nc.gpsimd.tensor_tensor(w2_gated[:, b], w2_sb[:, b],
                                        gates[:, 1:2, :].broadcast_to([P, IT, E]), ALU.mult).then_inc(w2_ready, 1)

            def split_w(b, e):
                for parts, w in ((w1_parts, w1_sb), (w3_parts, w3_sb)):
                    nc.gpsimd.tensor_copy(parts[:, b, 0], w[:, b]).then_inc(w_rounded, 1)
                for k, (parts, w) in enumerate(((w1_parts, w1_sb), (w3_parts, w3_sb))):
                    pool.wait_ge(w_rounded, 2 * e + 1 + k)
                    last = nc.gpsimd.tensor_tensor(parts[:, b, 1], w[:, b], parts[:, b, 0].bitcast(F32),
                                                   ALU.subtract)
                last.then_inc(w13_ready, 1)

            pool.wait_ge(mod_ready, 1)
            pool.wait_ge(ld_w[0], 48)
            split_w(0, 0)
            for r in range(CHUNKS):
                pool.wait_ge(hT_rounded, r + 1)
                tokens = slice(r * BANK, (r + 1) * BANK)
                nc.gpsimd.tensor_tensor(hT_lo[:, tokens], hT[:, r * TB:(r + 1) * TB, :].rearrange("p a b -> p (a b)"),
                                        hT_hi[:, tokens].bitcast(F32), ALU.subtract).then_inc(hT_split, 1)
            gate_w2(0)
            pool.wait_ge(ld_w[1], 48)
            split_w(1, 1)
            gate_w2(1)
            with pool.Fori(0, NX // 2 - 1) as turn:
                e0 = turn * 2
                for b in range(2):
                    pool.wait_ge(ld_w[b], e0 * 24 + 96)
                    pool.wait_ge(y_filled, (e0 + b + 1) * CHUNKS)
                    gate_w2(b)
                    split_w(b, e0 + b + 2)

        @block.scalar
        def _(act):
            act.wait_ge(ld_mod, 32)
            nc.scalar.activation(silu_c[:], c_sb[:, 0:1].broadcast_to([P, P]), ACT.Silu).then_inc(silu_c_ready, 1)

            def norm(k):
                act.wait_ge(var_ready, k + 1)
                nc.scalar.activation(rstd[:], moments[:, :, 1], ACT.Sqrt).then_inc(std_ready, 1)
                if k == 0:
                    act.wait_ge(modcol_ready, 1)
                for r in range(CHUNKS):
                    act.wait_ge(norm_transposed, k * CHUNKS + r + 1)
                    nc.scalar.activation(hT[:, r * TB:(r + 1) * TB, :].rearrange("p a b -> p (a b)"), PS[:, r, :],
                                         ACT.Identity, bias=modcol[:, 2 * k:2 * k + 1],
                                         scale=modcol[:, 2 * k + 1:2 * k + 2]).then_inc(hT_ready, 1)
                    if k == 1:
                        nc.scalar.activation(hT_hi[:, r * BANK:(r + 1) * BANK], PS[:, r, :],
                                             ACT.Identity, bias=modcol[:, 2:3], scale=modcol[:, 3:4])\
                          .then_inc(hT_rounded, 1)

            norm(0)

            def ring_to(n, dst, key, width, shape=None):
                slot = n.slot_at[key]
                act.wait_ge(ring_filled, slot + 1)
                src = PS[:, RING + slot % RING_BANKS, 0:width]
                if shape:
                    src = src.rearrange("p (a b) -> p a b", a=shape)
                nc.scalar.activation(dst, src, ACT.Copy).then_inc(ring_act, 1)

            def exps(n, x):
                _, J, q, r, m = x
                ch = J // PAIRS
                bank = SCORES + n.at[x] % SCORE_BANKS
                if q < ch:
                    k = quad_of[J, m, q]
                    if r == 0 and k in (QUADS - 2, QUADS - 1):
                        act.wait_ge(ring_filled, n.slot_at["rowsum", -1] + 1)
                    if r == 0 and k >= QUADS:
                        oJ, om, oq = quad_owner[k - QUADS]
                        if oq >= oJ // PAIRS - 1:
                            act.wait_ge(ring_filled, n.slot_at["rowsum", oJ] + 1)
                        else:
                            if ("poolsum", oJ, om, oq + 1) in n.at:
                                act.wait_ge(pool_added, n.at["poolsum", oJ, om, oq + 1] + 1)
                            else:
                                act.wait_ge(quad_added, n.at["quadsum", oJ, om, TB - 1] // TB + 1)
                    act.wait_ge(scores_ready, n.at[x] + 1)
                    nc.scalar.activation(full[:, k % QUADS, r, :], PS[:, bank, :], ACT.Exp).then_inc(probs_ready, 1)
                else:
                    if r == 0 and J > 0:
                        act.wait_ge(pv_done, n.at["pv", J - 1, (J - 1) // PAIRS, TB - 1] + 1)
                        if ("poolsum", J - 1, m, (J - 1) // PAIRS) in n.at:
                            act.wait_ge(pool_added, n.at["poolsum", J - 1, m, (J - 1) // PAIRS] + 1)
                        else:
                            act.wait_ge(diag_added, n.at["diagsum", J - 1, m, 1] // 2 + 1)
                    act.wait_ge(scores_ready, n.at[x] + 1)
                    nc.scalar.activation(diag[:, m, r, r * P:BANK], PS[:, bank, r * P:BANK], ACT.Exp)\
                      .then_inc(probs_ready, 1)

            def round_parts(n, x):
                b, ch = x[1] % TB, x[1] // TB
                act.wait_ge(rotated_ready, n.at[x] + 1)
                if ("k", x[1] - TB) in n.slot_at:
                    act.wait_ge(ring_filled, n.slot_at["k", x[1] - TB] + 1)
                q = rotated[:, b % 2, 0:QH * HEAD].rearrange("p (h n) -> p h n", n=HEAD)
                k = rotated[:, b % 2, QH * HEAD:QK].unsqueeze(1).broadcast_to([P, 2, HEAD])
                nc.scalar.copy(q_split[:, b, :, 0, :], q)
                nc.scalar.copy(k_split[:, b, 0, :].rearrange("p (a n) -> p a n", a=2), k).then_inc(parts_ready, 1)
                nc.scalar.copy(q_max[:, ch % 2, b, :, 0:HEAD], q).then_inc(q_max_ready, 1)

            def walk(n, ends):
                for x in n.order:
                    if x[0] == "low":
                        round_parts(n, x)
                    elif x[0] == "qk":
                        i = x[1] % TILES
                        ch, t = divmod(i, TB)
                        ring_to(n, QT[:, ch % 2, :, t * P:(t + 1) * P], ("q",) + x[1:], QH * P, QH)
                        ring_to(n, KT[:, :, i * P:(i + 1) * P], ("k",) + x[1:], 2 * P, 2)
                    elif x[0] == "qmax":
                        ring_to(n, QMT[:, 2 * (x[1] % PAIRS) + x[2], :], x, BANK)
                    elif x[0] == "s":
                        exps(n, x)
                    elif x[0] == "values":
                        nc.scalar.copy(V[:, 0:2 * TB, :], V_next[:]).then_inc(values_ready, 1)
                act.sem_inc(engine_through, 1)
                act.wait_ge(group_go, ends)

            act.wait_ge(pads_ready, 1)
            walk(lead, 1)
            with act.Fori(0, GROUPS) as g:
                walk(loop, g + 2)

            norm(1)
            act.wait_ge(logits_ready, 1)
            nc.scalar.activation(tok_w[:], logits[:], ACT.Exp).then_inc(exp_logits, 1)

            with act.Fori(0, NX // 2) as turn:
                e0 = turn * 2
                for u in range(2 * UNITS):
                    act.wait_ge(gu_filled, e0 * UNITS + u + 1)
                    nc.scalar.activation(silu_g[:, u % 2, :], PS[:, 2 * (u % 2), :], ACT.Silu).then_inc(silu_ready, 1)

        @block.vector
        def _(dve):
            chain = [0]

            def link(ins):
                chain[0] += 1
                ins.then_inc(dve_chain, 1)
                dve.wait_ge(dve_chain, chain[0])

            def tile_stats(source, tiles):
                for i in tiles:
                    last = nc.vector.bn_stats(stats[:, i, :], source[:, i, :])
                link(last)
                for i in tiles:
                    last = nc.vector.bn_aggr(moments[:, i, :], stats[:, i, :])
                link(last)

            def norm_scale(k):
                nc.vector.tensor_scalar(moments[:, :, 1], moments[:, :, 1], LN_EPS, None, ALU.add)\
                  .then_inc(var_ready, 1)
                dve.wait_ge(std_ready, k + 1)
                link(nc.vector.reciprocal(rstd[:], rstd[:]))

            def normalise(source, to):
                for i in range(TILES):
                    last = nc.vector.tensor_scalar(to[:, i, :], source[:, i, :], moments[:, i, 0:1], rstd[:, i:i + 1],
                                                   ALU.subtract, ALU.mult)
                    if i % TB == TB - 1:
                        last.then_inc(norm_ready, 1)

            def modulation():
                dve.wait_ge(mod_filled, 2)
                ga_gb = PS[:, AV:AV + 2, 2 * E:3 * E]
                link(nc.vector.tensor_copy(gates[:], ga_gb))
                link(nc.vector.scalar_tensor_tensor(out=gate_abs[:], in0=gates[:], scalar=-1.0, in1=gates[:],
                                                    op0=ALU.mult, op1=ALU.max))
                nc.vector.tensor_scalar(gate_abs[:], gate_abs[:], GATE_FLOOR, None, ALU.max)
                link(nc.vector.tensor_scalar(gate_sign[:], ga_gb, 0.0, 2.0, ALU.is_ge, ALU.mult))
                link(nc.vector.scalar_tensor_tensor(out=gates[:], in0=gate_sign[:], scalar=-1.0, in1=gate_abs[:],
                                                    op0=ALU.add, op1=ALU.mult))
                nc.vector.memset(PS[:, AV + 1, :], 0.0)
                link(nc.vector.tensor_tensor(gate_bo[:], gates[:, 0, :], bo_sb[:], ALU.mult))
                nc.vector.tensor_tensor(XA[:], X[:], gate_bo[:].unsqueeze(1).broadcast_to([P, TILES, E]), ALU.add)
                for g in range(1 + GROUPS):
                    last = nc.vector.tensor_tensor(wo_sb[:, g], wo_sb[:, g],
                                                   gates[:, 0:1, :].broadcast_to([P, PAIRS, E]), ALU.mult)
                last.then_inc(mod_ready, 1)

            dve.wait_ge(ld_x, 16)
            tile_stats(X, range(TILES))
            norm_scale(0)
            dve.wait_ge(mod_filled, 1)
            nc.vector.tensor_copy(modcol[:, 0:4:2], PS[:, 5, 0:4:2])
            nc.vector.tensor_scalar(modcol[:, 1:4:2], PS[:, 5, 1:4:2], 1.0, None, ALU.add).then_inc(modcol_ready, 1)
            normalise(X, normed[0])
            dve.wait_ge(ld_attn, 240)
            nc.vector.tensor_scalar(wqkv[:, :, 0:QH * HEAD], wqkv[:, :, 0:QH * HEAD], SCALE, None, ALU.mult)
            nc.vector.tensor_scalar(bqkv[:, :, 0:QH * HEAD], bqkv[:, :, 0:QH * HEAD], SCALE, None, ALU.mult)\
              .then_inc(q_scaled, 1)
            dve.wait_ge(ld_const, 80)
            nc.vector.tensor_copy(ident16[:], ident[:])
            nc.vector.tensor_copy(causal16[:], causal[:]).then_inc(masks_ready, 1)
            dve.wait_ge(q_scaled, 1)

            vlinks = [0]

            def vlink(ins):
                vlinks[0] += 1
                ins.then_inc(vector_chain, 1)
                dve.wait_ge(vector_chain, vlinks[0])

            def step(n, x, g):
                def ring_wait(key):
                    dve.wait_ge(ring_filled, n.slot_at[key] + 1)
                    return RING + n.slot_at[key] % RING_BANKS

                kind = x[0]
                if kind == "modulation":
                    modulation()
                elif kind == "proj":
                    i = x[1]
                    bank = ring_wait(x)
                    if n.at[x] >= 2:
                        dve.wait_ge(rotated_ready, n.at[x] - 1)
                    nc.vector.tensor_tensor(qkv_sb[:, i % 2, :], PS[:, bank, 0:QK],
                                            bqkv[:, bass.ds(g, 1), 0:QK].rearrange("p o n -> p (o n)"), ALU.add)\
                      .then_inc(proj_added, 1)
                    v = V[:, i, :] if i < TILES else V_next[:, i - TILES, :]
                    nc.vector.tensor_tensor(v, PS[:, bank, QK:QKV],
                                            bqkv[:, bass.ds(g, 1), QK:QKV].rearrange("p o n -> p (o n)"), ALU.add)\
                      .then_inc(ring_dve, 1)
                elif kind == "low":
                    b = x[1] % TB
                    dve.wait_ge(parts_ready, n.at[x] + 1)
                    nc.vector.tensor_tensor(q_split[:, b, :, 1, :],
                                            rotated[:, b % 2, 0:QH * HEAD].rearrange("p (h n) -> p h n", n=HEAD),
                                            q_split[:, b, :, 0, :].bitcast(F32), ALU.subtract)
                    nc.vector.tensor_tensor(k_split[:, b, 1, 0:HEAD], rotated[:, b % 2, QH * HEAD:QK],
                                            k_split[:, b, 0, 0:HEAD].bitcast(F32), ALU.subtract).then_inc(low_ready, 1)
                elif kind == "max":
                    _, J, m, t, b = x
                    ch = J % N_J // PAIRS
                    bank = ring_wait(x)
                    width = BANK if b < ch else (t + 1) * P
                    if ch == 0:
                        nc.vector.tensor_reduce(q_max[:, 0, t, 2 * (J % PAIRS) + m, HEAD:HEAD + 1],
                                                PS[:, bank, 0:width], AX.X, ALU.max, negate=True).then_inc(ring_dve, 1)
                    else:
                        nc.vector.reduce_max(part_max[:, t, b:b + 1], PS[:, bank, 0:width], AX.X).then_inc(ring_dve, 1)
                elif kind == "maxed":
                    _, J, m = x
                    ch = J % N_J // PAIRS
                    dve.wait_ge(ring_dve, n.emptied(("max", J, m, TB - 1, ch))[1])
                    if ch:
                        vlink(nc.vector.tensor_reduce(q_max[:, ch % 2, :, 2 * (J % PAIRS) + m, HEAD],
                                                      part_max[:, :, 0:ch + 1], AX.X, ALU.max, negate=True))
                    dve.sem_inc(max_ready, 1)
                elif kind == "quadsum":
                    _, J, m, k = x
                    q = CHUNKS - 2
                    if k == 0:
                        dve.wait_ge(pv_done, n.at["pv", J, q, TB - 1] + 1)
                        dve.wait_ge(pool_added, n.at["poolsum", J, m, q - 1] + 1)
                    a, b = quad_of[J, m, q] % QUADS, quad_of[J, m, q - 1] % QUADS
                    last = nc.vector.tensor_tensor(full[:, a, k], full[:, a, k], full[:, b, k], ALU.add)
                    if k == TB - 1:
                        last.then_inc(quad_added, 1)
                elif kind == "diagsum":
                    _, J, m, part = x
                    ch = J // PAIRS
                    acc = full[:, acc_quad(J, m)]
                    if part == 0:
                        dve.wait_ge(probs_ready, n.at["s", J, ch, TB - 1, m] + 1)
                        dve.wait_ge(quad_added, n.at["quadsum", J, m, TB - 1] // TB + 1)
                    for r in ((0, 3), (1, 2))[part]:
                        last = nc.vector.tensor_tensor(acc[:, r, r * P:BANK], acc[:, r, r * P:BANK],
                                                       diag[:, m, r, r * P:BANK], ALU.add)
                    if part == 1:
                        last.then_inc(diag_added, 1)
                elif kind == "sum":
                    _, J, m, piece = x
                    ch = J // PAIRS
                    acc = full[:, acc_quad(J, m)]
                    if piece == 0 and J >= 0:
                        if ("poolsum", J, m, ch) in n.at:
                            dve.wait_ge(pool_added, n.at["poolsum", J, m, ch] + 1)
                        else:
                            dve.wait_ge(diag_added, n.at["diagsum", J, m, 1] // 2 + 1)
                    if ch == 0:
                        if piece == 2:
                            nc.vector.tensor_tensor(acc[:, 0, 2 * P:BANK], acc[:, 0, 2 * P:BANK],
                                                    acc[:, 1, 2 * P:BANK], ALU.add).then_inc(sum_ready, 1)
                    elif piece < 2:
                        ins = nc.vector.tensor_tensor(acc[:, piece], acc[:, piece], acc[:, piece + 2], ALU.add)
                        if piece == 1:
                            vlink(ins)
                    else:
                        nc.vector.tensor_tensor(acc[:, 0], acc[:, 0], acc[:, 1], ALU.add).then_inc(sum_ready, 1)
                elif kind == "rowsum":
                    J = x[1]
                    bank = ring_wait(x)
                    nc.vector.transpose(sum_cols[:], PS[:, bank, :]).then_inc(ring_dve, 1)
                    dve.wait_ge(ring_dve, n.emptied(x)[1])
                    vlink(nc.vector.reciprocal(inv_cols[:], sum_cols[:, 0:BANK:32]))
                    vlink(nc.vector.transpose(inv_rows[:].rearrange("p (a b) -> p a b", b=32),
                                              inv_cols[:].unsqueeze(2).broadcast_to([P, BANK // 32, 32])))
                elif kind == "norm":
                    J = x[1]
                    if J >= 0:
                        dve.wait_ge(pv_done, n.at["pv", J, J // PAIRS, TB - 1] + 1)
                    nc.vector.tensor_tensor(attnT[:, J % PAIRS, :], PS[:, AV + J % 2, :], inv_rows[:], ALU.mult)\
                      .then_inc(attn_ready, 1)
                elif kind == "out":
                    bank = ring_wait(x)
                    ch = x[1]
                    i = ch % CHUNKS * TB
                    rows = XA[:, i:i + TB, :].rearrange("p a b -> p (a b)")
                    nc.vector.tensor_tensor(rows, rows, PS[:, bank, :], ALU.add).then_inc(ring_dve, 1)

            dve.wait_ge(pads_ready, 1)
            def walk(n, g, ends):
                vlinks[0] = 0
                for x in n.order:
                    step(n, x, g + 1 if x[0] == "proj" and x[1] >= TILES else g)
                dve.sem_inc(engine_through, 1)
                dve.wait_ge(group_go, ends)

            walk(lead, -1, 1)
            with dve.Fori(0, GROUPS) as g:
                walk(loop, g, g + 2)
            vlinks[0] = 0
            for x in last_out.order:
                if x[0] == "out":
                    tile_stats(XA, range(TILES - TB))
                step(last_out, x, GROUPS)
            dve.wait_ge(ring_dve, last_out.emptied(("out", -1))[1])
            tile_stats(XA, range(TILES - TB, TILES))
            norm_scale(1)
            normalise(XA, normed[1])
            dve.wait_ge(router_filled, 1)
            link(nc.vector.tensor_copy(logits[:], PS[:, 4, 0:TILES * NX].rearrange("p (t x) -> p t x", x=NX)))
            for j in range(NX):
                of_j = logits[:, :, j:j + 1]
                nc.vector.tensor_tensor(beats[:, :, 0:j + 1, j], of_j.broadcast_to([P, TILES, j + 1]),
                                        logits[:, :, 0:j + 1], ALU.is_gt)
                if j + 1 < NX:
                    nc.vector.tensor_tensor(beats[:, :, j + 1:NX, j], of_j.broadcast_to([P, TILES, NX - 1 - j]),
                                            logits[:, :, j + 1:NX], ALU.is_ge)
            link(nc.vector.reduce_max(best[:], logits[:], AX.X))
            nc.vector.tensor_tensor(logits[:], logits[:], best[:].unsqueeze(2).broadcast_to([P, TILES, NX]),
                                    ALU.subtract).then_inc(logits_ready, 1)
            link(nc.vector.tensor_reduce(rank[:].rearrange("p t x -> p (t x)"),
                                         beats[:].rearrange("p t a b -> p (t a) b"), AX.X, ALU.add))
            dve.wait_ge(exp_logits, 1)
            link(nc.vector.scalar_tensor_tensor(out=tok_w[:], in0=rank[:], scalar=1.5, in1=tok_w[:],
                                                op0=ALU.is_lt, op1=ALU.mult))
            link(nc.vector.reduce_sum(tok_sum[:], tok_w[:], AX.X))
            link(nc.vector.reciprocal(tok_sum[:], tok_sum[:]))
            link(nc.vector.tensor_tensor(tok_wT[:].rearrange("p x t -> p t x"), tok_w[:],
                                         tok_sum[:].unsqueeze(2).broadcast_to([P, TILES, NX]), ALU.mult))

            def gate_up(e0, u):
                dve.wait_ge(silu_ready, e0 * UNITS + u + 1)
                ch, it = divmod(u, IT)
                nc.vector.tensor_tensor(hidden[:, ch % 2, it, :], silu_g[:, u % 2, :], PS[:, 2 * (u % 2) + 1, :],
                                        ALU.mult).then_inc(hidden_ready, 1)

            def add_expert(e0, ch):
                dve.wait_ge(y_filled, e0 * CHUNKS + ch + 1)
                e = e0 + ch // CHUNKS
                for t in range(TB):
                    i = ch % CHUNKS * TB + t
                    nc.vector.scalar_tensor_tensor(
                        out=XA[:, i, :], in0=PS[:, 4 + ch % 2, t * P:(t + 1) * P],
                        scalar=tok_wT[:, bass.ds(e, 1), i:i + 1].rearrange("p o t -> p (o t)"), in1=XA[:, i, :],
                        op0=ALU.mult, op1=ALU.add).then_inc(y_added, 1)

            with dve.Fori(0, NX // 2) as turn:
                e0 = turn * 2
                for ch in range(2 * CHUNKS):
                    for it in range(IT):
                        gate_up(e0, ch * IT + it)
                        if it == 1 and ch >= 1:
                            add_expert(e0, ch - 1)
                add_expert(e0, 2 * CHUNKS - 1)

        @block.tensor
        def _(pe):
            pe.wait_ge(ld_mod, 32)
            pe.wait_ge(silu_c_ready, 1)
            for n, m in enumerate((0, 1, 3, 4)):
                last = nc.tensor.matmul(PS[:, 5, n:n + 1], wmod_sb[:, m * E:(m + 1) * E], silu_c[:, 0:1],
                                        start=True, stop=True)
            last.then_inc(mod_filled, 1)
            for m in range(2):
                last = nc.tensor.matmul(PS[:, AV + m, 0:3 * E], silu_c[:], wmod_sb[:, 3 * m * E:3 * (m + 1) * E],
                                        start=True, stop=True)
            last.then_inc(mod_filled, 1)

            def norm(k):
                if k == 0:
                    pe.wait_ge(ld_const, 80)
                for r in range(CHUNKS):
                    pe.wait_ge(norm_ready, k * CHUNKS + r + 1)
                    for t in range(TB):
                        last = nc.tensor.transpose(PS[:, r, t * P:(t + 1) * P], normed[k][:, r * TB + t, :], ident[:])
                    last.then_inc(norm_transposed, 1)

            norm(0)
            pe.wait_ge(hT_ready, CHUNKS)
            pe.wait_ge(masks_ready, 1)

            known = {}

            def need(s, value):
                if known.get(id(s), 0) < value:
                    known[id(s)] = value
                    pe.wait_ge(s, value)

            def step(n, x, g):
                def ring_bank(key):
                    k = n.slot_at[key]
                    if k >= RING_BANKS:
                        engine = n.engine_of[k - RING_BANKS]
                        need(ring_sem[engine], n.engine_of[:k - RING_BANKS + 1].count(engine))
                    return RING + k % RING_BANKS

                def taken(key):
                    if key in n.slot_at:
                        engine, count = n.emptied(key)
                        need(ring_sem[engine], count)

                kind = x[0]
                if kind == "proj":
                    nc.tensor.matmul(PS[:, ring_bank(x), 0:QKV], hT[:, x[1] % TILES, :],
                                     wqkv[:, bass.ds(g, 1), :].rearrange("p o n -> p (o n)"),
                                     start=True, stop=True).then_inc(ring_filled, 1)
                elif kind == "qk":
                    i = x[1]
                    need(low_ready, n.at["low", i] + 1)
                    bank = ring_bank(("q", i))
                    for h in range(QH):
                        last = nc.tensor.transpose(PS[:, bank, h * P:(h + 1) * P],
                                                   q_split[:, i % TB, h].rearrange("p a b -> p (a b)").bitcast(F32),
                                                   ident[:])
                    last.then_inc(ring_filled, 1)
                    bank = ring_bank(("k", i))
                    for m in range(2):
                        last = nc.tensor.transpose(PS[:, bank, m * P:(m + 1) * P], k_split[:, i % TB, m].bitcast(F32),
                                                   ident[:])
                    last.then_inc(ring_filled, 1)
                elif kind == "max":
                    _, J, m, t, b = x
                    taken(("k", J // PAIRS * TB + t))
                    ch, h = J % N_J // PAIRS, 2 * (J % PAIRS) + m
                    bank = ring_bank(x)
                    last_bank = b == ch
                    w = (t + 1) * P if last_bank else BANK
                    last = nc.tensor.matmul(PS[:, bank, 0:w], QT[:, ch % 2, h, t * P:(t + 1) * P],
                                            KT[:, 0, b * BANK:b * BANK + w], start=True, stop=not last_bank)
                    if last_bank:
                        last = nc.tensor.matmul(PS[:, bank, w - P:w], ident16[:], causal16[:, 0, :],
                                                start=False, stop=True)
                    last.then_inc(ring_filled, 1)
                elif kind == "qmax":
                    _, J, m = x
                    need(max_ready, n.at["maxed", J, m] + 1)
                    if ("low", J // PAIRS * TB + TB - 1) in n.at:
                        need(q_max_ready, n.at["low", J // PAIRS * TB + TB - 1] + 1)
                    bank = ring_bank(x)
                    for t in range(TB):
                        last = nc.tensor.transpose(PS[:, bank, t * P:(t + 1) * P],
                                                   q_max[:, J // PAIRS % 2, t, 2 * (J % PAIRS) + m, :].bitcast(F32),
                                                   ident[:])
                    last.then_inc(ring_filled, 1)
                elif kind == "s":
                    _, J, q, r, m = x
                    ch, h, k = J // PAIRS, 2 * (J % PAIRS) + m, n.at[x]
                    taken(("k", ch * TB + TB - 1))
                    taken(("qmax", J, m))
                    if k >= SCORE_BANKS:
                        need(probs_ready, k - SCORE_BANKS + 1)
                    kt = q * TB + r
                    q0 = r * P if q == ch else 0
                    bank = SCORES + k % SCORE_BANKS
                    o = PS[:, bank, q0:BANK]
                    nc.tensor.matmul(o, KT[:, 0, kt * P:(kt + 1) * P], QT[:, ch % 2, h, q0:BANK],
                                     start=True, stop=False)
                    last = nc.tensor.matmul(o, KT[:, 1, kt * P:(kt + 1) * P], QMT[:, h, q0:BANK],
                                            start=False, stop=q < ch)
                    if q == ch:
                        last = nc.tensor.matmul(PS[:, bank, q0:q0 + P], ident16[:], causal16[:, 1, :],
                                                start=False, stop=True)
                    last.then_inc(scores_ready, 1)
                elif kind == "pv":
                    _, J, q, r = x
                    ch = J // PAIRS
                    need(probs_ready, n.at["s", J, q, r, 1] + 1)
                    need(values_ready, 1)
                    if q == 0 and r == 0 and J >= 1:
                        need(attn_ready, n.at["norm", J - 2] + 1)
                    kt = q * TB + r
                    q0 = r * P if q == ch else 0
                    for m in range(2):
                        pT = full[:, quad_of[J, m, q] % QUADS, r, :] if q < ch else diag[:, m, r, q0:BANK]
                        last = nc.tensor.matmul(PS[HEAD * m:HEAD * (m + 1), AV + J % 2, q0:BANK], V[:, kt, :],
                                                pT, start=(kt == 0), stop=(kt == ch * TB + TB - 1))
                    last.then_inc(pv_done, 1)
                elif kind == "rowsum":
                    J = x[1]
                    need(sum_ready, 2 * n.at[x] + 2)
                    bank = ring_bank(x)
                    for m in range(2):
                        acc = full[:, acc_quad(J, m), 0, :]
                        last = nc.tensor.matmul(PS[HEAD * m:HEAD * (m + 1), bank, :], ones[:], acc,
                                                start=True, stop=True)
                    last.then_inc(ring_filled, 1)
                elif kind == "out":
                    ch = x[1]
                    need(attn_ready, n.at["norm", PAIRS * ch + PAIRS - 1] + 1)
                    bank = ring_bank(x)
                    for t in range(TB):
                        for j in range(PAIRS):
                            last = nc.tensor.matmul(PS[:, bank, t * P:(t + 1) * P], attnT[:, j, t * P:(t + 1) * P],
                                                    wo_sb[:, bass.ds(g + (ch >= 0), 1), j, :].rearrange("p o n -> p (o n)"),
                                                    start=(j == 0), stop=(j == PAIRS - 1))
                    last.then_inc(ring_filled, 1)

            pe.wait_ge(pads_ready, 1)
            pe.wait_ge(q_scaled, 1)
            def walk(n, g, ends):
                known.clear()
                for x in n.order:
                    step(n, x, g + 1 if x[0] == "proj" and x[1] >= TILES else g)
                pe.sem_inc(engine_through, 1)
                pe.wait_ge(group_go, ends)

            walk(lead, -1, 1)
            with pe.Fori(0, GROUPS) as g:
                walk(loop, g, g + 2)
            known.clear()
            for x in last_out.order:
                step(last_out, x, GROUPS)

            norm(1)
            pe.wait_ge(hT_ready, 2 * CHUNKS)
            for i in range(TILES):
                last = nc.tensor.matmul(PS[:, 4, i * NX:(i + 1) * NX], hT[:, i, :], gate_sb[:], start=True, stop=True)
            last.then_inc(router_filled, 1)
            pe.wait_ge(hT_split, CHUNKS)

            def gate_up(e0, u):
                b, it, ch = u // UNITS, u % IT, u % UNITS // IT
                if u % UNITS == 0:
                    pe.wait_ge(w13_ready, e0 + b + 1)
                if u >= 2:
                    pe.wait_ge(hidden_ready, e0 * UNITS + u - 1)
                for m, w in enumerate((w1_parts, w3_parts)):
                    for k, (part, h) in enumerate(((0, hT_hi), (0, hT_lo), (1, hT_hi))):
                        last = nc.tensor.matmul(PS[:, 2 * (u % 2) + m, :], w[:, b, part, it * P:(it + 1) * P],
                                                h[:, ch * BANK:(ch + 1) * BANK], start=(k == 0), stop=(k == 2))
                last.then_inc(gu_filled, 1)

            def down(e0, ch):
                b = ch // CHUNKS
                if ch % CHUNKS == 0:
                    pe.wait_ge(w2_ready, e0 + b + 1)
                pe.wait_ge(hidden_ready, e0 * UNITS + (ch + 1) * IT)
                if ch >= 2:
                    pe.wait_ge(y_added, e0 * TILES + (ch - 1) * TB)
                for t in range(TB):
                    for it in range(IT):
                        last = nc.tensor.matmul(PS[:, 4 + ch % 2, t * P:(t + 1) * P],
                                                hidden[:, ch % 2, it, t * P:(t + 1) * P], w2_gated[:, b, it, :],
                                                start=(it == 0), stop=(it == IT - 1))
                last.then_inc(y_filled, 1)

            with pe.Fori(0, NX // 2) as turn:
                e0 = turn * 2
                for ch in range(2 * CHUNKS):
                    for it in range(IT):
                        gate_up(e0, ch * IT + it)
                        if it == 1 and ch >= 1:
                            down(e0, ch - 1)
                down(e0, 2 * CHUNKS - 1)


_INS = ["L0_attn_x", "L0_attn_Wq", "L0_attn_bq", "L0_attn_Wk", "L0_attn_bk", "L0_attn_Wv", "L0_attn_bv",
        "L0_attn_Wo", "L0_attn_bo", "L0_ffn_gate", "L0_ffn_experts_w1", "L0_ffn_experts_w2",
        "L0_ffn_experts_w3", "L0_c", "L0_wmod"]
_OUTS = [((1, 2048, 128), "float32")]


def kernel(**inputs):
    import numpy as _np
    import concourse.bacc as _bacc
    from concourse import mybir as _mybir
    from concourse.bass_utils import run_bass_kernel_spmd as _run

    nc = _bacc.Bacc("TRN2", target_bir_lowering=False, num_devices=1)
    arrays, args = {}, []
    laid = {name: _np.ascontiguousarray(inputs[name]) for name in _INS}
    laid.update(constants(_OUTS[0][0][1]))
    for name, a in laid.items():
        arrays[f"in_{name}_dram"] = a
        args.append(nc.dram_tensor(f"in_{name}_dram", a.shape, _mybir.dt.from_np(a.dtype), kind="ExternalInput").ap())
    for i, (shape, dtype) in enumerate(_OUTS):
        dt = _mybir.dt.from_np(_np.dtype(dtype))
        args.append(nc.dram_tensor(f"out_{i}_dram", shape, dt, kind="ExternalOutput").ap())
    block_kernel(nc, *args)
    r = _run(nc, [arrays], core_ids=[0])
    return r.results[0]["out_0_dram"]
```

```python
from contextlib import ExitStack

import numpy as np

import concourse.bass as bass
from concourse import mybir

ALU = mybir.AluOpType
ACT = mybir.ActivationFunctionType
AX = mybir.AxisListType
F32 = mybir.dt.float32
F32R = mybir.dt.float32r
BF16 = mybir.dt.bfloat16

P = 128
BANK = 512
HEAD = 64
HALF = HEAD // 2
LN_EPS = 1e-5
GATE_FLOOR = 0.25
MASKED = -1e30
ROPE_BASE = 10000.0


def rotary_tables(tokens):
    inv_freq = (1.0 / np.float32(ROPE_BASE) ** (np.arange(0, HEAD, 2, dtype=np.float32) / np.float32(HEAD)))
    angle = np.arange(tokens, dtype=np.float32)[:, None] * inv_freq.astype(np.float32)[None, :]
    cos, sin = np.cos(angle).astype(np.float32), np.sin(angle).astype(np.float32)
    return cos, np.concatenate([-sin, sin], 1)


def constants(tokens):
    cos, sin = rotary_tables(tokens)
    row, col = np.arange(P)[:, None], np.arange(P)[None, :]
    return {
        "k_cos": cos,
        "k_sin": sin,
        "k_ident": np.eye(P, dtype=np.float32),
        "k_causal": np.stack([np.where(col <= row, 0.0, MASKED), np.where(row <= col, 0.0, MASKED)], 1)
        .astype(np.float32),
    }


def block_kernel(nc, x_in, Wq, bq, Wk, bk, Wv, bv, Wo, bo, gate, w1, w2, w3, c, wmod,
                 cos, sin, ident_in, causal_in, out):
    T, E = x_in.shape[1], x_in.shape[2]
    GROUPS = Wk.shape[1] // HEAD
    QH = Wq.shape[1] // HEAD // GROUPS
    PAIRS = QH // 2
    TILES = T // P
    QK = (QH + 1) * HEAD
    QKV = QK + HEAD
    NX, INNER = w1.shape[0], w1.shape[2]
    IT = INNER // P
    TB = BANK // P
    SCORE_BANKS, RING_BANKS = 2, 4
    CHUNKS = TILES // TB
    SCALE = float(HEAD) ** -0.5
    assert E == P and SCALE == 0.125 and QH == 4

    PAIR_STEPS = range(CHUNKS * PAIRS)
    N_J = CHUNKS * PAIRS

    def weight(x):
        if x[0] in ("s", "max"):
            _, J, m, t, b = x if x[0] == "max" else (x[0], x[1], x[4], x[3], x[2])
            part = 1.0 if b < J % N_J // PAIRS else ((t + 1) if x[0] == "max" else (TB - t)) / TB
            return part * (3.78 if x[0] == "max" else 2.0)
        return {"pv": 2.1, "qmax": 1.5, "proj": 3.0, "low": 3.0, "qk": 3.5, "poolsum": 0.01, "maxed": 0.25,
                "diagsum": 3.3, "quadsum": 0.01, "sum": 2.8, "rowsum": 12.6, "norm": 2.8, "modulation": 0.0,
                "out": 8.0}[x[0]]

    def maxima(J, m):
        return [("max", J, m, t, b) for t in range(TB) for b in range(J % N_J // PAIRS + 1)] + [("maxed", J, m)]

    def max_steps(J):
        first, second = maxima(J, 0), maxima(J, 1)
        return first + second[:3] + [("qmax", J, 0)] + second[3:]

    def parts(ch):
        i = ch * TB
        return [("proj", i), ("proj", i + 1), ("low", i), ("proj", i + 2), ("low", i + 1), ("proj", i + 3),
                ("low", i + 2), ("low", i + 3)]

    def turned(ch):
        return [("qk", ch * TB + t) for t in range(TB)]

    def tail_steps(J):
        steps = [("sum", J, m, piece) for m in range(2) for piece in range(3)]
        steps += [("rowsum", J), ("norm", J)]
        return steps + ([("out", J // PAIRS)] if J % PAIRS == PAIRS - 1 else [])

    def diag_steps(J):
        if J // PAIRS == CHUNKS - 1:
            return [("diagsum", J, m, part) for m in range(2) for part in range(2)]
        return [("poolsum", J, m, J // PAIRS) for m in range(2)]

    main = []
    starts, pending = [], []
    for J in PAIR_STEPS:
        starts.append(len(main))
        for q in range(J // PAIRS + 1):
            for r in range(TB):
                main += [("s", J, q, r, 0), ("s", J, q, r, 1)] + pending
                if r == 0 and q > 1:
                    if q < CHUNKS - 1:
                        main += [("poolsum", J, m, q - 1) for m in range(2)]
                    else:
                        main += [("quadsum", J, m, part) for m in range(2) for part in range(4)]
                pending = [("pv", J, q, r)]
    starts.append(len(main))
    before = np.cumsum([0.0] + [weight(x) for x in main])
    begin = [float(before[k]) for k in starts]
    begin.append(begin[-1] + 30.0)

    def place(items, lo, hi):
        at = [begin[int(x)] + (x % 1) * (begin[int(x) + 1] - begin[int(x)]) for x in (lo, hi)]
        ends = np.cumsum([weight(x) for x in items])
        return [(at[0] + (at[1] - at[0]) * float(end - weight(x) / 2) / float(ends[-1]), x)
                for x, end in zip(items, ends)]

    def merge(*placed):
        return [x for _, x in sorted((y for items in placed for y in items), key=lambda y: y[0])]

    end = N_J
    side = [
        place(maxima(2, 0), 0.05, 0.99),
        place([("qmax", 2, 0)] + maxima(2, 1), 1.01, 1.74),
        place(parts(2), 0.6, 2.59), place(turned(2), 2.59, 3.05), place(parts(3), 3.23, 4.08),
        place(turned(3), 3.84, 4.87),
        place(max_steps(3), 2.01, 2.95), place(max_steps(4), 2.82, 3.88), place(max_steps(5), 4.02, 4.88),
        place(max_steps(6), 4.89, 5.72), place(max_steps(7), 5.77, 6.8),
        place(parts(CHUNKS), 6.19, 7.16), place(turned(CHUNKS), 7.32, 7.47), place(max_steps(end), 7.4, 7.71),
        place(parts(CHUNKS + 1), 7.42, 8.14), place(maxima(end + 1, 0) + maxima(end + 1, 1), 7.77, 7.85),
        place([("qmax", end, 1)], 7.71, 7.79),
        place(turned(CHUNKS + 1), 8.0, 8.36), place([("qmax", end + 1, m) for m in range(2)], 8.4, 8.7),
        place(diag_steps(5), 6.05, 6.1), place(tail_steps(5), 6.22, 6.84),
        place(diag_steps(6) + tail_steps(6), 7.0, 7.48),
        place(tail_steps(-1), 0.02, 1.1), place(diag_steps(7), 8.01, 8.38),
    ] + [place([("qmax", J, 1)], J - 0.03, J - 0.02) for J in range(2, N_J)]\
      + [place(diag_steps(J), J + 1.02, J + 1.1) for J in range(5)]\
      + [place(tail_steps(J), J + 1.36, J + 2.02) for J in range(5)]
    closing = tail_steps(-1)
    body = [("values",)] + merge([(float(b), x) for b, x in zip(before, main)], [(begin[end], x) for x in pending],
                                 *side)
    lead_in = []
    maxima_first = max_steps(end) + [("qmax", end, 1)] + max_steps(end + 1) + [("qmax", end + 1, 1)]
    for k in range(2 * TB + 2):
        i = TILES + k
        lead_in += [("proj", i)] * (k < 2 * TB) + [("low", i - 1)] * (0 < k <= 2 * TB) + [("qk", i - 2)] * (k > 1)
        if k % 2 and k // 2 in range(1, 4):
            lead_in.append(("modulation", k // 2 - 1))
        if k > TB + 1:
            n = len(maxima_first) // TB if k < 2 * TB + 1 else len(maxima_first)
            lead_in += maxima_first[:n]
            maxima_first = maxima_first[n:]

    class Counts:

        def __init__(self, order):
            self.order = order
            self.at = {}
            number = {}
            for x in order:
                self.at[x] = number.setdefault(x[0], 0)
                number[x[0]] += 1
            self.number = number
            self.slot_at, self.engine_of = {}, []
            for x in order:
                for key, engine in {
                    "proj": [(x, "dve")], "qk": [(("q",) + x[1:], "act"), (("k",) + x[1:], "act")],
                    "max": [(x, "dve")], "qmax": [(x, "act")], "rowsum": [(x, "dve")],
                    "out": [(x, "dve")],
                }.get(x[0], []):
                    self.slot_at[key] = len(self.engine_of)
                    self.engine_of.append(engine)
            self.vector_links = sum((x[0] == "maxed" and x[1] % N_J >= PAIRS)
                                    + (x[0] == "sum" and x[1] not in range(PAIRS) and x[3] == 1)
                                    + 2 * (x[0] == "rowsum")
                                    for x in order)

        def emptied(self, key):
            n = self.slot_at[key]
            return self.engine_of[n], self.engine_of[:n + 1].count(self.engine_of[n])

    QUADS = 7
    quad_of, quad_owner = {}, []
    for x in body:
        if x[0] == "s" and x[3] == 0:
            _, J, q, _, m = x
            if q < J // PAIRS or q == 0:
                quad_of[J, m, q] = len(quad_owner)
                quad_owner.append((J, m, q))

    def acc_quad(J, m):
        J = J % N_J
        return quad_of[J, m, max(J // PAIRS - 1, 0)] % QUADS

    assert len(quad_owner) % QUADS == 0

    with ExitStack() as ctx:
        def sb(name, shape, dt=F32):
            return ctx.enter_context(nc.sbuf_tensor(name, shape, dt))

        def sem(name):
            return ctx.enter_context(nc.semaphore(name))

        PS = ctx.enter_context(nc.psum_tensor("PS", [P, 8, BANK], F32))
        SCORES, RING, AV = 0, 2, 6

        ident = sb("ident", [P, P])
        ident16 = sb("ident16", [P, P], BF16)
        causal16 = sb("causal16", [P, 2, P], BF16)
        cos_sb = sb("cos_sb", [P, TILES, HALF])
        sin_sb = sb("sin_sb", [P, TILES, HEAD])
        wqkv = sb("wqkv", [P, GROUPS + 1, QKV])
        bqkv = sb("bqkv", [P, GROUPS + 1, QKV])
        wo_sb = sb("wo_sb", [P, 1 + GROUPS, PAIRS, E])
        c_sb = sb("c_sb", [P, 1])
        ones = sb("ones", [P, HEAD])
        gate_sb = sb("gate_sb", [P, NX])
        modcol = sb("modcol", [P, 4])
        gates = sb("gates", [P, 2, E])
        XA = sb("XA", [P, TILES, E])
        hT = sb("hT", [P, TILES, P])
        stats = sb("stats", [P, TILES, 6])
        moments = sb("moments", [P, TILES, 2])
        rstd = sb("rstd", [P, TILES])
        qkv_sb = sb("qkv_sb", [P, 2, QK])
        rot_cos = sb("rot_cos", [P, QK])
        rot_sin = sb("rot_sin", [P, QK])
        rotated = sb("rotated", [P, 2, QK])
        q_split = sb("q_split", [P, TB, QH, 2, HEAD], F32R)
        k_split = sb("k_split", [P, TB, 2, P], F32R)
        q_max = sb("q_max", [P, 2, TB, QH, P], F32R)
        QT = sb("QT", [P, 2, QH, BANK], F32R)
        QMT = sb("QMT", [P, QH, BANK], F32R)
        KT = sb("KT", [P, 2, T], F32R)
        V = sb("V", [P, TILES, HEAD])
        V_next = sb("V_next", [P, 2 * TB, HEAD])
        part_max = sb("part_max", [P, TB, CHUNKS])
        sum_cols = sb("sum_cols", [P, BANK])
        inv_cols = sb("inv_cols", [P, BANK // 32])
        inv_rows = sb("inv_rows", [P, BANK])
        attnT = sb("attnT", [P, PAIRS, BANK])
        full = sb("full", [P, QUADS, TB, BANK])
        diag = sb("diag", [P, 2, TB, BANK])
        X = full[:, 0].rearrange("p a b -> p (a b)").rearrange("p (i e) -> p i e", e=E)
        normed = [full[:, n].rearrange("p a b -> p (a b)").rearrange("p (i e) -> p i e", e=E)
                  for n in (3, 0)]
        wmod_sb = full[:, 1].rearrange("p a b -> p (a b)")[:, 0:6 * E]
        causal = full[:, 2, 0, 0:2 * P].rearrange("p (a b) -> p a b", b=P)
        silu_c, bo_sb, gate_bo = (full[:, 2, 1, n * P:(n + 1) * P] for n in range(3))
        gate_abs, gate_sign = (full[:, 2, 2, n * 2 * E:(n + 1) * 2 * E].rearrange("p (a b) -> p a b", b=E)
                               for n in range(2))
        hidden = full[:, 1:3]
        weights = full[:, 3:5].rearrange("p n a b -> p n (a b)")
        w1_sb, w3_sb = weights[:, :, 0:INNER], weights[:, :, INNER:2 * INNER]
        w2_sb = weights[:, :, 2 * INNER:2 * INNER + IT * E].rearrange("p n (t e) -> p n t e", e=E)
        w2_gated = weights[:, :, 3 * INNER:3 * INNER + IT * E].rearrange("p n (t e) -> p n t e", e=E)
        silu_g = full[:, 5, 0:2, :]
        hT_hi, hT_lo = KT[:, 0, :], KT[:, 1, :]
        w1_parts = QT[:, 0].rearrange("p (n a) b -> p n a b", a=2)
        w3_parts = QMT[:].rearrange("p (n a) b -> p n a b", a=2)
        beats = full[:, 6].rearrange("p a b -> p (a b)")[:, 0:TILES * NX * NX]\
            .rearrange("p (t a b) -> p t a b", a=NX, b=NX)
        logits, rank, tok_w = (full[:, 5, 3, n * TILES * NX:(n + 1) * TILES * NX]
                               .rearrange("p (t x) -> p t x", x=NX) for n in range(3))
        best = sb("best", [P, TILES])
        tok_sum = sb("tok_sum", [P, TILES])
        tok_wT = sb("tok_wT", [P, NX, TILES])

        ld_x, ld_mod, ld_const, ld_attn = (
            sem("ld_x"), sem("ld_mod"), sem("ld_const"), sem("ld_attn"))
        dve_chain, silu_c_ready, mod_filled, mod_ready = (
            sem("dve_chain"), sem("silu_c_ready"), sem("mod_filled"), sem("mod_ready"))
        var_ready, std_ready, norm_ready = sem("var_ready"), sem("std_ready"), sem("norm_ready")
        norm_transposed, hT_ready = sem("norm_transposed"), sem("hT_ready")
        q_scaled, masks_ready, modcol_ready = sem("q_scaled"), sem("masks_ready"), sem("modcol_ready")
        proj_added, pool_chain, rotated_ready, pool_added = (
            sem("proj_added"), sem("pool_chain"), sem("rotated_ready"), sem("pool_added"))
        ring_filled, ring_act, ring_dve, vector_chain = (
            sem("ring_filled"), sem("ring_act"), sem("ring_dve"), sem("vector_chain"))
        max_ready, scores_ready, probs_ready, pv_done = (
            sem("max_ready"), sem("scores_ready"), sem("probs_ready"), sem("pv_done"))
        diag_added, sum_ready, attn_ready = sem("diag_added"), sem("sum_ready"), sem("attn_ready")
        quad_added = sem("quad_added")
        engine_through, group_go, pads_ready, values_ready = (
            sem("engine_through"), sem("group_go"), sem("pads_ready"), sem("values_ready"))
        parts_ready, low_ready, q_max_ready = sem("parts_ready"), sem("low_ready"), sem("q_max_ready")
        router_filled, logits_ready, exp_logits = sem("router_filled"), sem("logits_ready"), sem("exp_logits")
        ld_w = [sem("ld_w0"), sem("ld_w1")]
        w2_ready, w13_ready = sem("w2_ready"), sem("w13_ready")
        hT_rounded, hT_split, w_rounded = sem("hT_rounded"), sem("hT_split"), sem("w_rounded")
        gu_filled, silu_ready, hidden_ready = sem("gu_filled"), sem("silu_ready"), sem("hidden_ready")
        y_filled, y_added = sem("y_filled"), sem("y_added")
        stored = sem("stored")

        block = ctx.enter_context(nc.Block())

        POOL_OPS = 4

        def loop_sems(n):
            k = n.number
            return [
                (proj_added, k.get("proj", 0)), (pool_chain, POOL_OPS * k.get("proj", 0)),
                (rotated_ready, k.get("proj", 0)), (pool_added, k.get("poolsum", 0)),
                (diag_added, k.get("diagsum", 0) // 2),
                (quad_added, k.get("quadsum", 0) // TB),
                (ring_filled, len(n.engine_of)), (ring_act, n.engine_of.count("act")),
                (ring_dve, n.engine_of.count("dve")), (vector_chain, n.vector_links),
                (max_ready, k.get("maxed", 0)), (scores_ready, k.get("s", 0)), (probs_ready, k.get("s", 0)),
                (pv_done, k.get("pv", 0)), (sum_ready, k.get("sum", 0) // 3),
                (attn_ready, k.get("norm", 0)), (values_ready, k.get("values", 0)),
                (parts_ready, k.get("low", 0)), (low_ready, k.get("low", 0)), (q_max_ready, k.get("low", 0)),
            ]

        ring_sem = {"act": ring_act, "dve": ring_dve}

        lead, loop, last_out = Counts(lead_in), Counts(body), Counts(closing)

        NORM_PASSES = [(0, range(CHUNKS)), (1, range(CHUNKS - 1)), (1, range(CHUNKS - 1, CHUNKS))]

        def tiles_of(chunks):
            return slice(chunks[0] * TB, (chunks[-1] + 1) * TB)

        UNITS = CHUNKS * IT

        @block.sync
        def _(sp):
            sp.dma_start(X[:], x_in[0].rearrange("(i p) e -> p i e", p=P)).then_inc(ld_x, 16)
            sp.dma_start(wmod_sb[:], wmod).then_inc(ld_mod, 16)
            sp.dma_start(c_sb[:], c.rearrange("a e -> e a")).then_inc(ld_mod, 16)
            sp.dma_start(ident[:], ident_in).then_inc(ld_const, 16)
            sp.dma_start(causal[:], causal_in).then_inc(ld_const, 16)
            sp.dma_start(bo_sb[:], bo.partition_broadcast(P)).then_inc(ld_const, 16)
            sp.dma_start(wo_sb[:, 1:1 + GROUPS], Wo.rearrange("(g j p) e -> p g j e", p=P, j=PAIRS))\
              .then_inc(ld_const, 16)
            sp.dma_start(gate_sb[:], gate).then_inc(ld_const, 16)

            def load_expert(e, b):
                sp.dma_start(w1_sb[:, b, :], w1[bass.ds(e, 1)].rearrange("o h i -> h (o i)")).then_inc(ld_w[b], 16)
                sp.dma_start(w3_sb[:, b, :], w3[bass.ds(e, 1)].rearrange("o h i -> h (o i)")).then_inc(ld_w[b], 16)
                sp.dma_start(w2_sb[:, b, :, :], w2[bass.ds(e, 1)].rearrange("o (t p) h -> p (o t) h", p=P))\
                  .then_inc(ld_w[b], 16)

            def end_walk(n):
                for s, count in loop_sems(n):
                    if count:
                        sp.wait_ge(s, count)
                sp.wait_ge(engine_through, 4)
                for s, count in loop_sems(n):
                    if count:
                        sp.sem_clear(s)
                sp.sem_clear(engine_through)
                sp.sem_inc(group_go, 1)

            end_walk(lead)
            with sp.Fori(0, GROUPS) as g:
                end_walk(loop)

            for b in range(2):
                load_expert(b, b)

            with sp.Fori(0, NX // 2 - 1) as turn:
                e0 = turn * 2
                for b in range(2):
                    sp.wait_ge(y_filled, (e0 + b + 1) * CHUNKS)
                    load_expert(e0 + 2 + b, b)
            for ch in range(CHUNKS):
                sp.wait_ge(y_added, (NX - 1) * TILES + (ch + 1) * TB)
                sp.dma_start(out[0].rearrange("(i p) e -> p i e", p=P)[:, ch * TB:(ch + 1) * TB],
                             XA[:, ch * TB:(ch + 1) * TB]).then_inc(stored, 16)
            sp.wait_ge(stored, CHUNKS * 16)

        @block.gpsimd
        def _(pool):
            chain = [0]

            def link(ins):
                chain[0] += 1
                ins.then_inc(pool_chain, 1)
                return chain[0]

            nc.gpsimd.memset(wqkv[:, GROUPS, :], 0.0)
            nc.gpsimd.memset(bqkv[:, GROUPS, :], 0.0)
            nc.gpsimd.memset(wo_sb[:, 0], 0.0)
            nc.gpsimd.memset(ones[:], 1.0)
            nc.gpsimd.memset(k_split[:, :, 1, HEAD:HEAD + 1].bitcast(F32), 1.0)
            nc.gpsimd.memset(k_split[:, :, 1, HEAD + 1:P].bitcast(F32), 0.0)
            nc.gpsimd.memset(q_max[:, :, :, :, HEAD + 1:P].bitcast(F32), 0.0)
            for r in range(1, TB):
                nc.gpsimd.memset(diag[:, :, r, 0:r * P], 0.0)
            for m in range(2):
                nc.gpsimd.memset(full[:, acc_quad(-1, m)], 1.0)
            nc.gpsimd.memset(attnT[:], 0.0).then_inc(pads_ready, 1)
            pool.wait_ge(ld_attn, 128)

            def walk(n, ends):
                chain[0] = 0
                for x in n.order:
                    if x[0] == "proj":
                        rotary(n, x)
                    elif x[0] == "poolsum":
                        _, J, m, q = x
                        ch = J // PAIRS
                        if q > 1:
                            pool.wait_ge(pool_added, n.at["poolsum", J, m, q - 1] + 1)
                        if q < ch:
                            pool.wait_ge(pv_done, n.at["pv", J, q, TB - 1] + 1)
                            a, b = quad_of[J, m, q] % QUADS, quad_of[J, m, q - 1] % QUADS
                            nc.gpsimd.tensor_tensor(full[:, a], full[:, a], full[:, b], ALU.add)\
                              .then_inc(pool_added, 1)
                            continue
                        pool.wait_ge(probs_ready, n.at["s", J, ch, TB - 1, m] + 1)
                        acc = full[:, acc_quad(J, m)]
                        if ch:
                            pool.wait_ge(pv_done, n.at["pv", J, ch - 1, TB - 1] + 1)
                            for r in range(TB):
                                last = nc.gpsimd.tensor_tensor(acc[:, r, r * P:BANK], acc[:, r, r * P:BANK],
                                                               diag[:, m, r, r * P:BANK], ALU.add)
                        else:
                            for r in range(0, TB, 2):
                                last = nc.gpsimd.tensor_tensor(acc[:, r // 2, r * P:BANK], diag[:, m, r, r * P:BANK],
                                                               diag[:, m, r + 1, r * P:BANK], ALU.add)
                        last.then_inc(pool_added, 1)
                pool.sem_inc(engine_through, 1)
                pool.wait_ge(group_go, ends)

            def rotary(n, x):
                i = x[1] % TILES
                pool.wait_ge(proj_added, n.at[x] + 1)
                if n.at[x] >= 2:
                    pool.wait_ge(low_ready, n.at[x] - 1)
                    pool.wait_ge(q_max_ready, n.at[x] - 1)
                qk = qkv_sb[:, i % 2, :].rearrange("p (h n) -> p h n", n=HEAD)
                rc = rot_cos[:].rearrange("p (h n) -> p h n", n=HEAD)
                rs = rot_sin[:].rearrange("p (h n) -> p h n", n=HEAD)
                ro = rotated[:, i % 2].rearrange("p (h n) -> p h n", n=HEAD)
                halves = 2 * (QH + 1)
                link(nc.gpsimd.tensor_tensor(rot_cos[:].rearrange("p (h n) -> p h n", n=HALF),
                                             qkv_sb[:, i % 2, :].rearrange("p (h n) -> p h n", n=HALF),
                                             cos_sb[:, i:i + 1, :].broadcast_to([P, halves, HALF]), ALU.mult))
                for lo, hi in ((0, HALF), (HALF, HEAD)):
                    sn = sin_sb[:, i:i + 1, lo:hi].broadcast_to([P, QH + 1, HALF])
                    done = link(nc.gpsimd.tensor_tensor(rs[:, :, lo:hi], qk[:, :, HALF - lo:HEAD - lo], sn, ALU.mult))
                pool.wait_ge(pool_chain, done)
                done = link(nc.gpsimd.tensor_tensor(ro, rc, rs, ALU.add))
                assert chain[0] == POOL_OPS * (n.at[x] + 1)
                pool.wait_ge(pool_chain, done)
                pool.sem_inc(rotated_ready, 1)

            walk(lead, 1)
            with pool.Fori(0, GROUPS) as g:
                walk(loop, g + 2)

            def gate_w2(b):
                nc.gpsimd.tensor_tensor(w2_gated[:, b], w2_sb[:, b],
                                        gates[:, 1:2, :].broadcast_to([P, IT, E]), ALU.mult).then_inc(w2_ready, 1)

            def split_w(b, e):
                for parts, w in ((w1_parts, w1_sb), (w3_parts, w3_sb)):
                    nc.gpsimd.tensor_copy(parts[:, b, 0], w[:, b]).then_inc(w_rounded, 1)
                for k, (parts, w) in enumerate(((w1_parts, w1_sb), (w3_parts, w3_sb))):
                    pool.wait_ge(w_rounded, 2 * e + 1 + k)
                    last = nc.gpsimd.tensor_tensor(parts[:, b, 1], w[:, b], parts[:, b, 0].bitcast(F32),
                                                   ALU.subtract)
                last.then_inc(w13_ready, 1)

            pool.wait_ge(mod_ready, 1)
            pool.wait_ge(ld_w[0], 48)
            split_w(0, 0)
            for r in range(CHUNKS):
                pool.wait_ge(hT_rounded, r + 1)
                tokens = slice(r * BANK, (r + 1) * BANK)
                nc.gpsimd.tensor_tensor(hT_lo[:, tokens], hT[:, r * TB:(r + 1) * TB, :].rearrange("p a b -> p (a b)"),
                                        hT_hi[:, tokens].bitcast(F32), ALU.subtract).then_inc(hT_split, 1)
            gate_w2(0)
            pool.wait_ge(ld_w[1], 48)
            split_w(1, 1)
            gate_w2(1)
            with pool.Fori(0, NX // 2 - 1) as turn:
                e0 = turn * 2
                for b in range(2):
                    pool.wait_ge(ld_w[b], e0 * 24 + 96)
                    pool.wait_ge(y_filled, (e0 + b + 1) * CHUNKS)
                    gate_w2(b)
                    split_w(b, e0 + b + 2)

        @block.scalar
        def _(act):
            for w, b, at in ((Wq, bq, slice(0, QH * HEAD)), (Wk, bk, slice(QH * HEAD, QK)), (Wv, bv, slice(QK, QKV))):
                act.dma_start(wqkv[:, 0:GROUPS, at], w.rearrange("e (g n) -> e g n", g=GROUPS)).then_inc(ld_attn, 16)
                act.dma_start(bqkv[:, 0:GROUPS, at], b.rearrange("(g n) -> g n", g=GROUPS).partition_broadcast(P))\
                   .then_inc(ld_attn, 16)
            act.dma_start(cos_sb[:], cos.rearrange("(i p) d -> p i d", p=P)).then_inc(ld_attn, 16)
            act.dma_start(sin_sb[:], sin.rearrange("(i p) d -> p i d", p=P)).then_inc(ld_attn, 16)
            act.wait_ge(ld_mod, 32)
            nc.scalar.activation(silu_c[:], c_sb[:, 0:1].broadcast_to([P, P]), ACT.Silu).then_inc(silu_c_ready, 1)

            def norm(n):
                k, chunks = NORM_PASSES[n]
                act.wait_ge(var_ready, n + 1)
                nc.scalar.activation(rstd[:, tiles_of(chunks)], moments[:, tiles_of(chunks), 1], ACT.Sqrt)\
                  .then_inc(std_ready, 1)
                if k == 0:
                    act.wait_ge(modcol_ready, 1)
                for r in chunks:
                    act.wait_ge(norm_transposed, k * CHUNKS + r + 1)
                    nc.scalar.activation(hT[:, r * TB:(r + 1) * TB, :].rearrange("p a b -> p (a b)"), PS[:, r, :],
                                         ACT.Identity, bias=modcol[:, 2 * k:2 * k + 1],
                                         scale=modcol[:, 2 * k + 1:2 * k + 2]).then_inc(hT_ready, 1)
                    if k == 1:
                        nc.scalar.activation(hT_hi[:, r * BANK:(r + 1) * BANK], PS[:, r, :],
                                             ACT.Identity, bias=modcol[:, 2:3], scale=modcol[:, 3:4])\
                          .then_inc(hT_rounded, 1)

            norm(0)

            def ring_to(n, dst, key, width, shape=None):
                slot = n.slot_at[key]
                act.wait_ge(ring_filled, slot + 1)
                src = PS[:, RING + slot % RING_BANKS, 0:width]
                if shape:
                    src = src.rearrange("p (a b) -> p a b", a=shape)
                nc.scalar.activation(dst, src, ACT.Copy).then_inc(ring_act, 1)

            def exps(n, x):
                _, J, q, r, m = x
                ch = J // PAIRS
                bank = SCORES + n.at[x] % SCORE_BANKS
                if q < ch:
                    k = quad_of[J, m, q]
                    if r == 0 and k in (QUADS - 2, QUADS - 1):
                        act.wait_ge(ring_filled, n.slot_at["rowsum", -1] + 1)
                    if r == 0 and k >= QUADS:
                        oJ, om, oq = quad_owner[k - QUADS]
                        if oq >= oJ // PAIRS - 1:
                            act.wait_ge(ring_filled, n.slot_at["rowsum", oJ] + 1)
                        else:
                            if ("poolsum", oJ, om, oq + 1) in n.at:
                                act.wait_ge(pool_added, n.at["poolsum", oJ, om, oq + 1] + 1)
                            else:
                                act.wait_ge(quad_added, n.at["quadsum", oJ, om, TB - 1] // TB + 1)
                    act.wait_ge(scores_ready, n.at[x] + 1)
                    nc.scalar.activation(full[:, k % QUADS, r, :], PS[:, bank, :], ACT.Exp).then_inc(probs_ready, 1)
                else:
                    if r == 0 and J > 0:
                        act.wait_ge(pv_done, n.at["pv", J - 1, (J - 1) // PAIRS, TB - 1] + 1)
                        if ("poolsum", J - 1, m, (J - 1) // PAIRS) in n.at:
                            act.wait_ge(pool_added, n.at["poolsum", J - 1, m, (J - 1) // PAIRS] + 1)
                        else:
                            act.wait_ge(diag_added, n.at["diagsum", J - 1, m, 1] // 2 + 1)
                    act.wait_ge(scores_ready, n.at[x] + 1)
                    nc.scalar.activation(diag[:, m, r, r * P:BANK], PS[:, bank, r * P:BANK], ACT.Exp)\
                      .then_inc(probs_ready, 1)

            def round_parts(n, x):
                b, ch = x[1] % TB, x[1] // TB
                act.wait_ge(rotated_ready, n.at[x] + 1)
                if ("k", x[1] - TB) in n.slot_at:
                    act.wait_ge(ring_filled, n.slot_at["k", x[1] - TB] + 1)
                q = rotated[:, b % 2, 0:QH * HEAD].rearrange("p (h n) -> p h n", n=HEAD)
                k = rotated[:, b % 2, QH * HEAD:QK].unsqueeze(1).broadcast_to([P, 2, HEAD])
                nc.scalar.copy(q_split[:, b, :, 0, :], q)
                nc.scalar.copy(k_split[:, b, 0, :].rearrange("p (a n) -> p a n", a=2), k).then_inc(parts_ready, 1)
                nc.scalar.copy(q_max[:, ch % 2, b, :, 0:HEAD], q).then_inc(q_max_ready, 1)

            def walk(n, ends):
                for x in n.order:
                    if x[0] == "low":
                        round_parts(n, x)
                    elif x[0] == "qk":
                        i = x[1] % TILES
                        ch, t = divmod(i, TB)
                        ring_to(n, QT[:, ch % 2, :, t * P:(t + 1) * P], ("q",) + x[1:], QH * P, QH)
                        ring_to(n, KT[:, :, i * P:(i + 1) * P], ("k",) + x[1:], 2 * P, 2)
                    elif x[0] == "qmax":
                        ring_to(n, QMT[:, 2 * (x[1] % PAIRS) + x[2], :], x, BANK)
                    elif x[0] == "s":
                        exps(n, x)
                    elif x[0] == "values":
                        nc.scalar.copy(V[:, 0:2 * TB, :], V_next[:]).then_inc(values_ready, 1)
                act.sem_inc(engine_through, 1)
                act.wait_ge(group_go, ends)

            act.wait_ge(pads_ready, 1)
            walk(lead, 1)
            with act.Fori(0, GROUPS) as g:
                walk(loop, g + 2)

            norm(1)
            norm(2)
            act.wait_ge(logits_ready, 1)
            nc.scalar.activation(tok_w[:], logits[:], ACT.Exp).then_inc(exp_logits, 1)

            with act.Fori(0, NX // 2) as turn:
                e0 = turn * 2
                for u in range(2 * UNITS):
                    act.wait_ge(gu_filled, e0 * UNITS + u + 1)
                    nc.scalar.activation(silu_g[:, u % 2, :], PS[:, 2 * (u % 2), :], ACT.Silu).then_inc(silu_ready, 1)

        @block.vector
        def _(dve):
            chain = [0]

            def link(ins):
                chain[0] += 1
                ins.then_inc(dve_chain, 1)
                dve.wait_ge(dve_chain, chain[0])

            def tile_stats(source, tiles):
                for i in tiles:
                    last = nc.vector.bn_stats(stats[:, i, :], source[:, i, :])
                link(last)
                for i in tiles:
                    last = nc.vector.bn_aggr(moments[:, i, :], stats[:, i, :])
                link(last)

            def norm_scale(n):
                t = tiles_of(NORM_PASSES[n][1])
                nc.vector.tensor_scalar(moments[:, t, 1], moments[:, t, 1], LN_EPS, None, ALU.add)\
                  .then_inc(var_ready, 1)
                dve.wait_ge(std_ready, n + 1)
                link(nc.vector.reciprocal(rstd[:, t], rstd[:, t]))

            def normalise(source, to, n):
                for r in NORM_PASSES[n][1]:
                    for i in range(r * TB, (r + 1) * TB):
                        last = nc.vector.tensor_scalar(to[:, i, :], source[:, i, :], moments[:, i, 0:1],
                                                       rstd[:, i:i + 1], ALU.subtract, ALU.mult)
                    last.then_inc(norm_ready, 1)

            def modulation(part):
                if part == 0:
                    dve.wait_ge(mod_filled, 2)
                    ga_gb = PS[:, AV:AV + 2, 2 * E:3 * E]
                    link(nc.vector.tensor_copy(gates[:], ga_gb))
                    link(nc.vector.scalar_tensor_tensor(out=gate_abs[:], in0=gates[:], scalar=-1.0, in1=gates[:],
                                                        op0=ALU.mult, op1=ALU.max))
                    nc.vector.tensor_scalar(gate_abs[:], gate_abs[:], GATE_FLOOR, None, ALU.max)
                    link(nc.vector.tensor_scalar(gate_sign[:], ga_gb, 0.0, 2.0, ALU.is_ge, ALU.mult))
                    link(nc.vector.scalar_tensor_tensor(out=gates[:], in0=gate_sign[:], scalar=-1.0, in1=gate_abs[:],
                                                        op0=ALU.add, op1=ALU.mult))
                    nc.vector.memset(PS[:, AV + 1, :], 0.0)
                    link(nc.vector.tensor_tensor(gate_bo[:], gates[:, 0, :], bo_sb[:], ALU.mult))
                elif part == 1:
                    nc.vector.tensor_tensor(XA[:], X[:], gate_bo[:].unsqueeze(1).broadcast_to([P, TILES, E]), ALU.add)
                else:
                    for g in range(1, 1 + GROUPS):
                        last = nc.vector.tensor_tensor(wo_sb[:, g], wo_sb[:, g],
                                                       gates[:, 0:1, :].broadcast_to([P, PAIRS, E]), ALU.mult)
                    last.then_inc(mod_ready, 1)

            dve.wait_ge(ld_x, 16)
            tile_stats(X, range(TILES))
            norm_scale(0)
            dve.wait_ge(mod_filled, 1)
            nc.vector.tensor_copy(modcol[:, 0:4:2], PS[:, 5, 0:4:2])
            nc.vector.tensor_scalar(modcol[:, 1:4:2], PS[:, 5, 1:4:2], 1.0, None, ALU.add).then_inc(modcol_ready, 1)
            normalise(X, normed[0], 0)
            dve.wait_ge(ld_attn, 128)
            for t in (wqkv, bqkv):
                q_cols = t[:, 0:GROUPS, 0:QH * HEAD]
                last = nc.vector.tensor_scalar(q_cols, q_cols, SCALE, None, ALU.mult)
            last.then_inc(q_scaled, 1)
            dve.wait_ge(ld_const, 80)
            nc.vector.tensor_copy(ident16[:], ident[:])
            nc.vector.tensor_copy(causal16[:], causal[:]).then_inc(masks_ready, 1)
            dve.wait_ge(q_scaled, 1)

            vlinks = [0]

            def vlink(ins):
                vlinks[0] += 1
                ins.then_inc(vector_chain, 1)
                dve.wait_ge(vector_chain, vlinks[0])

            def step(n, x, g):
                def ring_wait(key):
                    dve.wait_ge(ring_filled, n.slot_at[key] + 1)
                    return RING + n.slot_at[key] % RING_BANKS

                kind = x[0]
                if kind == "modulation":
                    modulation(x[1])
                elif kind == "proj":
                    i = x[1]
                    bank = ring_wait(x)
                    if n.at[x] >= 2:
                        dve.wait_ge(rotated_ready, n.at[x] - 1)
                    nc.vector.tensor_tensor(qkv_sb[:, i % 2, :], PS[:, bank, 0:QK],
                                            bqkv[:, bass.ds(g, 1), 0:QK].rearrange("p o n -> p (o n)"), ALU.add)\
                      .then_inc(proj_added, 1)
                    v = V[:, i, :] if i < TILES else V_next[:, i - TILES, :]
                    nc.vector.tensor_tensor(v, PS[:, bank, QK:QKV],
                                            bqkv[:, bass.ds(g, 1), QK:QKV].rearrange("p o n -> p (o n)"), ALU.add)\
                      .then_inc(ring_dve, 1)
                elif kind == "low":
                    b = x[1] % TB
                    dve.wait_ge(parts_ready, n.at[x] + 1)
                    nc.vector.tensor_tensor(q_split[:, b, :, 1, :],
                                            rotated[:, b % 2, 0:QH * HEAD].rearrange("p (h n) -> p h n", n=HEAD),
                                            q_split[:, b, :, 0, :].bitcast(F32), ALU.subtract)
                    nc.vector.tensor_tensor(k_split[:, b, 1, 0:HEAD], rotated[:, b % 2, QH * HEAD:QK],
                                            k_split[:, b, 0, 0:HEAD].bitcast(F32), ALU.subtract).then_inc(low_ready, 1)
                elif kind == "max":
                    _, J, m, t, b = x
                    ch = J % N_J // PAIRS
                    bank = ring_wait(x)
                    width = BANK if b < ch else (t + 1) * P
                    if ch == 0:
                        nc.vector.tensor_reduce(q_max[:, 0, t, 2 * (J % PAIRS) + m, HEAD:HEAD + 1],
                                                PS[:, bank, 0:width], AX.X, ALU.max, negate=True).then_inc(ring_dve, 1)
                    else:
                        nc.vector.reduce_max(part_max[:, t, b:b + 1], PS[:, bank, 0:width], AX.X).then_inc(ring_dve, 1)
                elif kind == "maxed":
                    _, J, m = x
                    ch = J % N_J // PAIRS
                    dve.wait_ge(ring_dve, n.emptied(("max", J, m, TB - 1, ch))[1])
                    if ch:
                        vlink(nc.vector.tensor_reduce(q_max[:, ch % 2, :, 2 * (J % PAIRS) + m, HEAD],
                                                      part_max[:, :, 0:ch + 1], AX.X, ALU.max, negate=True))
                    dve.sem_inc(max_ready, 1)
                elif kind == "quadsum":
                    _, J, m, k = x
                    q = CHUNKS - 2
                    if k == 0:
                        dve.wait_ge(pv_done, n.at["pv", J, q, TB - 1] + 1)
                        dve.wait_ge(pool_added, n.at["poolsum", J, m, q - 1] + 1)
                    a, b = quad_of[J, m, q] % QUADS, quad_of[J, m, q - 1] % QUADS
                    last = nc.vector.tensor_tensor(full[:, a, k], full[:, a, k], full[:, b, k], ALU.add)
                    if k == TB - 1:
                        last.then_inc(quad_added, 1)
                elif kind == "diagsum":
                    _, J, m, part = x
                    ch = J // PAIRS
                    acc = full[:, acc_quad(J, m)]
                    if part == 0:
                        dve.wait_ge(probs_ready, n.at["s", J, ch, TB - 1, m] + 1)
                        dve.wait_ge(quad_added, n.at["quadsum", J, m, TB - 1] // TB + 1)
                    for r in ((0, 3), (1, 2))[part]:
                        last = nc.vector.tensor_tensor(acc[:, r, r * P:BANK], acc[:, r, r * P:BANK],
                                                       diag[:, m, r, r * P:BANK], ALU.add)
                    if part == 1:
                        last.then_inc(diag_added, 1)
                elif kind == "sum":
                    _, J, m, piece = x
                    ch = J // PAIRS
                    acc = full[:, acc_quad(J, m)]
                    if piece == 0 and J >= 0:
                        if ("poolsum", J, m, ch) in n.at:
                            dve.wait_ge(pool_added, n.at["poolsum", J, m, ch] + 1)
                        else:
                            dve.wait_ge(diag_added, n.at["diagsum", J, m, 1] // 2 + 1)
                    if ch == 0:
                        if piece == 2:
                            nc.vector.tensor_tensor(acc[:, 0, 2 * P:BANK], acc[:, 0, 2 * P:BANK],
                                                    acc[:, 1, 2 * P:BANK], ALU.add).then_inc(sum_ready, 1)
                    elif piece < 2:
                        ins = nc.vector.tensor_tensor(acc[:, piece], acc[:, piece], acc[:, piece + 2], ALU.add)
                        if piece == 1:
                            vlink(ins)
                    else:
                        nc.vector.tensor_tensor(acc[:, 0], acc[:, 0], acc[:, 1], ALU.add).then_inc(sum_ready, 1)
                elif kind == "rowsum":
                    J = x[1]
                    bank = ring_wait(x)
                    nc.vector.transpose(sum_cols[:], PS[:, bank, :]).then_inc(ring_dve, 1)
                    dve.wait_ge(ring_dve, n.emptied(x)[1])
                    vlink(nc.vector.reciprocal(inv_cols[:], sum_cols[:, 0:BANK:32]))
                    vlink(nc.vector.transpose(inv_rows[:].rearrange("p (a b) -> p a b", b=32),
                                              inv_cols[:].unsqueeze(2).broadcast_to([P, BANK // 32, 32])))
                elif kind == "norm":
                    J = x[1]
                    if J >= 0:
                        dve.wait_ge(pv_done, n.at["pv", J, J // PAIRS, TB - 1] + 1)
                    nc.vector.tensor_tensor(attnT[:, J % PAIRS, :], PS[:, AV + J % 2, :], inv_rows[:], ALU.mult)\
                      .then_inc(attn_ready, 1)
                elif kind == "out":
                    bank = ring_wait(x)
                    ch = x[1]
                    i = ch % CHUNKS * TB
                    rows = XA[:, i:i + TB, :].rearrange("p a b -> p (a b)")
                    nc.vector.tensor_tensor(rows, rows, PS[:, bank, :], ALU.add).then_inc(ring_dve, 1)

            dve.wait_ge(pads_ready, 1)

            def walk(n, g, ends):
                vlinks[0] = 0
                for x in n.order:
                    step(n, x, g + 1 if x[0] == "proj" and x[1] >= TILES else g)
                dve.sem_inc(engine_through, 1)
                dve.wait_ge(group_go, ends)

            walk(lead, -1, 1)
            with dve.Fori(0, GROUPS) as g:
                walk(loop, g, g + 2)
            vlinks[0] = 0
            for x in last_out.order:
                if x[0] == "rowsum":
                    tile_stats(XA, range(TILES - TB))
                    norm_scale(1)
                elif x[0] == "out":
                    normalise(XA, normed[1], 1)
                step(last_out, x, GROUPS)
            dve.wait_ge(ring_dve, last_out.emptied(("out", -1))[1])
            tile_stats(XA, range(TILES - TB, TILES))
            norm_scale(2)
            normalise(XA, normed[1], 2)
            dve.wait_ge(router_filled, 1)
            link(nc.vector.tensor_copy(logits[:], PS[:, 5, 0:TILES * NX].rearrange("p (t x) -> p t x", x=NX)))
            for j in range(NX):
                of_j = logits[:, :, j:j + 1]
                nc.vector.tensor_tensor(beats[:, :, 0:j + 1, j], of_j.broadcast_to([P, TILES, j + 1]),
                                        logits[:, :, 0:j + 1], ALU.is_gt)
                if j + 1 < NX:
                    nc.vector.tensor_tensor(beats[:, :, j + 1:NX, j], of_j.broadcast_to([P, TILES, NX - 1 - j]),
                                            logits[:, :, j + 1:NX], ALU.is_ge)
            link(nc.vector.reduce_max(best[:], logits[:], AX.X))
            nc.vector.tensor_tensor(logits[:], logits[:], best[:].unsqueeze(2).broadcast_to([P, TILES, NX]),
                                    ALU.subtract).then_inc(logits_ready, 1)
            link(nc.vector.tensor_reduce(rank[:].rearrange("p t x -> p (t x)"),
                                         beats[:].rearrange("p t a b -> p (t a) b"), AX.X, ALU.add))
            dve.wait_ge(exp_logits, 1)
            link(nc.vector.scalar_tensor_tensor(out=tok_w[:], in0=rank[:], scalar=1.5, in1=tok_w[:],
                                                op0=ALU.is_lt, op1=ALU.mult))
            link(nc.vector.reduce_sum(tok_sum[:], tok_w[:], AX.X))
            link(nc.vector.reciprocal(tok_sum[:], tok_sum[:]))
            link(nc.vector.tensor_tensor(tok_wT[:].rearrange("p x t -> p t x"), tok_w[:],
                                         tok_sum[:].unsqueeze(2).broadcast_to([P, TILES, NX]), ALU.mult))

            def gate_up(e0, u):
                dve.wait_ge(silu_ready, e0 * UNITS + u + 1)
                ch, it = divmod(u, IT)
                nc.vector.tensor_tensor(hidden[:, ch % 2, it, :], silu_g[:, u % 2, :], PS[:, 2 * (u % 2) + 1, :],
                                        ALU.mult).then_inc(hidden_ready, 1)

            def add_expert(e0, ch):
                dve.wait_ge(y_filled, e0 * CHUNKS + ch + 1)
                e = e0 + ch // CHUNKS
                for t in range(TB):
                    i = ch % CHUNKS * TB + t
                    nc.vector.scalar_tensor_tensor(
                        out=XA[:, i, :], in0=PS[:, 4 + ch % 2, t * P:(t + 1) * P],
                        scalar=tok_wT[:, bass.ds(e, 1), i:i + 1].rearrange("p o t -> p (o t)"), in1=XA[:, i, :],
                        op0=ALU.mult, op1=ALU.add).then_inc(y_added, 1)

            def turn_of(e0, last_turn):
                for ch in range(2 * CHUNKS):
                    for it in range(2 if ch == 0 else 0, IT):
                        gate_up(e0, ch * IT + it)
                    if ch >= 1:
                        add_expert(e0, ch - 1)
                if not last_turn:
                    gate_up(e0 + 2, 0)
                    gate_up(e0 + 2, 1)
                add_expert(e0, 2 * CHUNKS - 1)

            gate_up(0, 0)
            gate_up(0, 1)
            with dve.Fori(0, NX // 2 - 1) as turn:
                turn_of(turn * 2, False)
            turn_of(NX - 2, True)

        @block.tensor
        def _(pe):
            pe.wait_ge(ld_mod, 32)
            pe.wait_ge(silu_c_ready, 1)
            for n, m in enumerate((0, 1, 3, 4)):
                last = nc.tensor.matmul(PS[:, 5, n:n + 1], wmod_sb[:, m * E:(m + 1) * E], silu_c[:, 0:1],
                                        start=True, stop=True)
            last.then_inc(mod_filled, 1)
            for m in range(2):
                last = nc.tensor.matmul(PS[:, AV + m, 0:3 * E], silu_c[:], wmod_sb[:, 3 * m * E:3 * (m + 1) * E],
                                        start=True, stop=True)
            last.then_inc(mod_filled, 1)

            def norm(n):
                k, chunks = NORM_PASSES[n]
                if k == 0:
                    pe.wait_ge(ld_const, 80)
                for r in chunks:
                    pe.wait_ge(norm_ready, k * CHUNKS + r + 1)
                    for t in range(TB):
                        last = nc.tensor.transpose(PS[:, r, t * P:(t + 1) * P], normed[k][:, r * TB + t, :], ident[:])
                    last.then_inc(norm_transposed, 1)

            norm(0)
            pe.wait_ge(hT_ready, CHUNKS)
            pe.wait_ge(masks_ready, 1)

            known = {}

            def need(s, value):
                if known.get(id(s), 0) < value:
                    known[id(s)] = value
                    pe.wait_ge(s, value)

            def step(n, x, g):
                def ring_bank(key):
                    k = n.slot_at[key]
                    if k >= RING_BANKS:
                        engine = n.engine_of[k - RING_BANKS]
                        need(ring_sem[engine], n.engine_of[:k - RING_BANKS + 1].count(engine))
                    return RING + k % RING_BANKS

                def taken(key):
                    if key in n.slot_at:
                        engine, count = n.emptied(key)
                        need(ring_sem[engine], count)

                kind = x[0]
                if kind == "proj":
                    nc.tensor.matmul(PS[:, ring_bank(x), 0:QKV], hT[:, x[1] % TILES, :],
                                     wqkv[:, bass.ds(g, 1), :].rearrange("p o n -> p (o n)"),
                                     start=True, stop=True).then_inc(ring_filled, 1)
                elif kind == "qk":
                    i = x[1]
                    need(low_ready, n.at["low", i] + 1)
                    bank = ring_bank(("q", i))
                    for h in range(QH):
                        last = nc.tensor.transpose(PS[:, bank, h * P:(h + 1) * P],
                                                   q_split[:, i % TB, h].rearrange("p a b -> p (a b)").bitcast(F32),
                                                   ident[:])
                    last.then_inc(ring_filled, 1)
                    bank = ring_bank(("k", i))
                    for m in range(2):
                        last = nc.tensor.transpose(PS[:, bank, m * P:(m + 1) * P], k_split[:, i % TB, m].bitcast(F32),
                                                   ident[:])
                    last.then_inc(ring_filled, 1)
                elif kind == "max":
                    _, J, m, t, b = x
                    taken(("k", J // PAIRS * TB + t))
                    ch, h = J % N_J // PAIRS, 2 * (J % PAIRS) + m
                    bank = ring_bank(x)
                    last_bank = b == ch
                    w = (t + 1) * P if last_bank else BANK
                    last = nc.tensor.matmul(PS[:, bank, 0:w], QT[:, ch % 2, h, t * P:(t + 1) * P],
                                            KT[:, 0, b * BANK:b * BANK + w], start=True, stop=not last_bank)
                    if last_bank:
                        last = nc.tensor.matmul(PS[:, bank, w - P:w], ident16[:], causal16[:, 0, :],
                                                start=False, stop=True)
                    last.then_inc(ring_filled, 1)
                elif kind == "qmax":
                    _, J, m = x
                    need(max_ready, n.at["maxed", J, m] + 1)
                    if ("low", J // PAIRS * TB + TB - 1) in n.at:
                        need(q_max_ready, n.at["low", J // PAIRS * TB + TB - 1] + 1)
                    bank = ring_bank(x)
                    for t in range(TB):
                        last = nc.tensor.transpose(PS[:, bank, t * P:(t + 1) * P],
                                                   q_max[:, J // PAIRS % 2, t, 2 * (J % PAIRS) + m, :].bitcast(F32),
                                                   ident[:])
                    last.then_inc(ring_filled, 1)
                elif kind == "s":
                    _, J, q, r, m = x
                    ch, h, k = J // PAIRS, 2 * (J % PAIRS) + m, n.at[x]
                    taken(("k", ch * TB + TB - 1))
                    taken(("qmax", J, m))
                    if k >= SCORE_BANKS:
                        need(probs_ready, k - SCORE_BANKS + 1)
                    kt = q * TB + r
                    q0 = r * P if q == ch else 0
                    bank = SCORES + k % SCORE_BANKS
                    o = PS[:, bank, q0:BANK]
                    nc.tensor.matmul(o, KT[:, 0, kt * P:(kt + 1) * P], QT[:, ch % 2, h, q0:BANK],
                                     start=True, stop=False)
                    last = nc.tensor.matmul(o, KT[:, 1, kt * P:(kt + 1) * P], QMT[:, h, q0:BANK],
                                            start=False, stop=q < ch)
                    if q == ch:
                        last = nc.tensor.matmul(PS[:, bank, q0:q0 + P], ident16[:], causal16[:, 1, :],
                                                start=False, stop=True)
                    last.then_inc(scores_ready, 1)
                elif kind == "pv":
                    _, J, q, r = x
                    ch = J // PAIRS
                    need(probs_ready, n.at["s", J, q, r, 1] + 1)
                    need(values_ready, 1)
                    if q == 0 and r == 0 and J >= 1:
                        need(attn_ready, n.at["norm", J - 2] + 1)
                    kt = q * TB + r
                    q0 = r * P if q == ch else 0
                    for m in range(2):
                        pT = full[:, quad_of[J, m, q] % QUADS, r, :] if q < ch else diag[:, m, r, q0:BANK]
                        last = nc.tensor.matmul(PS[HEAD * m:HEAD * (m + 1), AV + J % 2, q0:BANK], V[:, kt, :],
                                                pT, start=(kt == 0), stop=(kt == ch * TB + TB - 1))
                    last.then_inc(pv_done, 1)
                elif kind == "rowsum":
                    J = x[1]
                    need(sum_ready, 2 * n.at[x] + 2)
                    bank = ring_bank(x)
                    for m in range(2):
                        acc = full[:, acc_quad(J, m), 0, :]
                        last = nc.tensor.matmul(PS[HEAD * m:HEAD * (m + 1), bank, :], ones[:], acc,
                                                start=True, stop=True)
                    last.then_inc(ring_filled, 1)
                elif kind == "out":
                    ch = x[1]
                    need(attn_ready, n.at["norm", PAIRS * ch + PAIRS - 1] + 1)
                    bank = ring_bank(x)
                    for t in range(TB):
                        for j in range(PAIRS):
                            last = nc.tensor.matmul(PS[:, bank, t * P:(t + 1) * P], attnT[:, j, t * P:(t + 1) * P],
                                                    wo_sb[:, bass.ds(g + (ch >= 0), 1), j, :]
                                                    .rearrange("p o n -> p (o n)"),
                                                    start=(j == 0), stop=(j == PAIRS - 1))
                    last.then_inc(ring_filled, 1)

            pe.wait_ge(pads_ready, 1)
            pe.wait_ge(q_scaled, 1)

            def walk(n, g, ends):
                known.clear()
                for x in n.order:
                    step(n, x, g + 1 if x[0] == "proj" and x[1] >= TILES else g)
                pe.sem_inc(engine_through, 1)
                pe.wait_ge(group_go, ends)

            walk(lead, -1, 1)
            with pe.Fori(0, GROUPS) as g:
                walk(loop, g, g + 2)
            known.clear()
            for x in last_out.order:
                step(last_out, x, GROUPS)

            for n in (1, 2):
                norm(n)
                for r in NORM_PASSES[n][1]:
                    pe.wait_ge(hT_ready, CHUNKS + r + 1)
                    for i in range(r * TB, (r + 1) * TB):
                        last = nc.tensor.matmul(PS[:, 5, i * NX:(i + 1) * NX], hT[:, i, :], gate_sb[:],
                                                start=True, stop=True)
            last.then_inc(router_filled, 1)
            pe.wait_ge(hT_split, CHUNKS)

            def gate_up(e0, u, first=False):
                b, it, ch = u // UNITS, u % IT, u % UNITS // IT
                if u % UNITS == 0:
                    pe.wait_ge(w13_ready, e0 + b + 1)
                if not first:
                    pe.wait_ge(hidden_ready, e0 * UNITS + u - 1)
                for m, w in enumerate((w1_parts, w3_parts)):
                    for k, (part, h) in enumerate(((0, hT_hi), (0, hT_lo), (1, hT_hi))):
                        last = nc.tensor.matmul(PS[:, 2 * (u % 2) + m, :], w[:, b, part, it * P:(it + 1) * P],
                                                h[:, ch * BANK:(ch + 1) * BANK], start=(k == 0), stop=(k == 2))
                last.then_inc(gu_filled, 1)

            def down(e0, ch, tiles):
                b = ch // CHUNKS
                if tiles[0] == 0:
                    if ch % CHUNKS == 0:
                        pe.wait_ge(w2_ready, e0 + b + 1)
                    pe.wait_ge(hidden_ready, e0 * UNITS + (ch + 1) * IT)
                    if ch >= 2:
                        pe.wait_ge(y_added, e0 * TILES + (ch - 1) * TB)
                for t in tiles:
                    for it in range(IT):
                        last = nc.tensor.matmul(PS[:, 4 + ch % 2, t * P:(t + 1) * P],
                                                hidden[:, ch % 2, it, t * P:(t + 1) * P], w2_gated[:, b, it, :],
                                                start=(it == 0), stop=(it == IT - 1))
                if tiles[-1] == TB - 1:
                    last.then_inc(y_filled, 1)

            after = {1: [0], 2: [1], 3: [2, 3]}

            def turn_of(e0, last_turn):
                for ch in range(2 * CHUNKS):
                    for it in range(2 if ch == 0 else 0, IT):
                        gate_up(e0, ch * IT + it)
                        if ch >= 1 and it in after:
                            down(e0, ch - 1, after[it])
                if not last_turn:
                    gate_up(e0 + 2, 0)
                    gate_up(e0 + 2, 1)
                down(e0, 2 * CHUNKS - 1, range(TB))

            gate_up(0, 0, first=True)
            gate_up(0, 1, first=True)
            with pe.Fori(0, NX // 2 - 1) as turn:
                turn_of(turn * 2, False)
            turn_of(NX - 2, True)


_INS = ["L0_attn_x", "L0_attn_Wq", "L0_attn_bq", "L0_attn_Wk", "L0_attn_bk", "L0_attn_Wv", "L0_attn_bv",
        "L0_attn_Wo", "L0_attn_bo", "L0_ffn_gate", "L0_ffn_experts_w1", "L0_ffn_experts_w2",
        "L0_ffn_experts_w3", "L0_c", "L0_wmod"]
_OUTS = [((1, 2048, 128), "float32")]


def kernel(**inputs):
    import numpy as _np
    import concourse.bacc as _bacc
    from concourse import mybir as _mybir
    from concourse.bass_utils import run_bass_kernel_spmd as _run

    nc = _bacc.Bacc("TRN2", target_bir_lowering=False, num_devices=1)
    arrays, args = {}, []
    laid = {name: _np.ascontiguousarray(inputs[name]) for name in _INS}
    laid.update(constants(_OUTS[0][0][1]))
    for name, a in laid.items():
        arrays[f"in_{name}_dram"] = a
        args.append(nc.dram_tensor(f"in_{name}_dram", a.shape, _mybir.dt.from_np(a.dtype), kind="ExternalInput").ap())
    for i, (shape, dtype) in enumerate(_OUTS):
        dt = _mybir.dt.from_np(_np.dtype(dtype))
        args.append(nc.dram_tensor(f"out_{i}_dram", shape, dt, kind="ExternalOutput").ap())
    block_kernel(nc, *args)
    r = _run(nc, [arrays], core_ids=[0])
    return r.results[0]["out_0_dram"]
```
